# Optimizing a Trainium2 kernel written in Bass

```python
import numpy as np
import jax
import jax.numpy as jnp

def _softmax(x, axis=-1):
    return jax.nn.softmax(x, axis=axis)

def _gelu(x):
    return jax.nn.gelu(x, approximate=True)

def _silu(x):
    return jax.nn.silu(x)

def _sigmoid(x):
    return jax.nn.sigmoid(x)

def _layernorm(x, axis=-1, eps=1e-05):
    m = jnp.mean(x, axis=axis, keepdims=True)
    v = jnp.var(x, axis=axis, keepdims=True)
    return (x - m) / jnp.sqrt(v + eps)

def _scatter_add(tgt, idx, src, axis=0):
    return tgt.at[idx].add(src)

def _segment_sum(src, seg, n):
    return jax.ops.segment_sum(src, seg, n)
kernel_name = 'mk_xattn_ffn_d1_seqx_r4_d18965'

def setup_inputs(seed: int=0):
    np.random.seed(seed)
    _w = jnp.asarray

    def _rec_inputs():
        import jax
        import jax.numpy as jnp
        _rk = jax.random.key(seed)
        x = 7.22e-05 + 1 * jax.random.normal(jax.random.fold_in(_rk, 1), (4, 512, 512), jnp.float32)
        _lenS = 512 - jax.random.randint(jax.random.fold_in(_rk, 7), (4,), 0, max(1, 512 // 4) + 1, jnp.int32)
        _lenS2 = 512 - jax.random.randint(jax.random.fold_in(_rk, 8), (4,), 0, max(1, 512 // 4) + 1, jnp.int32)
        _ctx_1024P = jax.random.normal(jax.random.fold_in(_rk, 11), (4, 16, 256), jnp.float32)
        _ctx_1024c = jax.random.dirichlet(jax.random.fold_in(_rk, 511), 0.3 * jnp.ones((16,), jnp.float32), (4, 512))
        _ctx_1024t = jnp.einsum('bsk,bkd->bsd', _ctx_1024c, _ctx_1024P)
        _ctx_1024t = _ctx_1024t * jax.lax.rsqrt(jnp.mean(jnp.square(_ctx_1024t)) + 1e-12) * 0.953939
        ctx_1024 = 2.81802e-05 + 1.00001 * (_ctx_1024t + 0.3 * jax.random.normal(jax.random.fold_in(_rk, 611), (4, 512, 256), jnp.float32))
        return (x, ctx_1024)
    x, ctx_1024 = _rec_inputs()

    def _L0_xattn_setup():
        import jax, jax.numpy as jnp
        import numpy as np
        key = jax.random.key(seed)
        ks = jax.random.split(key, 6)
        B, L, N, C, D = (8, 128, 512, 256, 128)
        return {'teacher_logits': jax.random.normal(ks[0], (B, L, N), dtype=jnp.float32), 'teacher_features': jax.random.normal(ks[1], (B, N, C), dtype=jnp.float32), 'Wq': jax.random.normal(ks[2], (D, C), dtype=jnp.float32) * (1.0 / np.sqrt(C)), 'bq': jnp.zeros((D,), dtype=jnp.float32), 'Wk': jax.random.normal(ks[3], (D, C), dtype=jnp.float32) * (1.0 / np.sqrt(C)), 'bk': jnp.zeros((D,), dtype=jnp.float32)}
    _L0_xattn_all = _L0_xattn_setup()
    _L0_xattn_in = {k: v for k, v in _L0_xattn_all.items() if k in ('Wq', 'bq', 'Wk', 'bk')}
    del _L0_xattn_all

    def _L0_ffn_setup():
        import jax, jax.numpy as jnp
        import numpy as np
        _FP8_MAX = 448.0
        _BLOCK = 32
        _EPS = 1e-30

        def _mx_dequant(t):
            rows, feat = t.shape
            blocks = t.reshape(rows, feat // _BLOCK, _BLOCK)
            max_abs = jnp.max(jnp.abs(blocks), axis=-1)
            scales = jnp.maximum(max_abs / _FP8_MAX, _EPS)
            q = (blocks / scales[..., None]).astype(jnp.float8_e4m3fn).astype(jnp.float32)
            return (q * scales[..., None]).reshape(rows, feat)

        def _mx_linear(x2d, w):
            return _mx_dequant(x2d) @ _mx_dequant(w).T
        key = jax.random.key(seed)
        k1, k2, k3, k4 = jax.random.split(key, 4)
        B, S, H, I = (2, 256, 512, 2048)
        return {'x': jax.random.normal(k1, (B, S, H), dtype=jnp.float32), 'gate_w': jax.random.normal(k2, (I, H), dtype=jnp.float32) * 0.02, 'up_w': jax.random.normal(k3, (I, H), dtype=jnp.float32) * 0.02, 'down_w': jax.random.normal(k4, (H, I), dtype=jnp.float32) * 0.02}
    _L0_ffn_all = _L0_ffn_setup()
    _L0_ffn_in = {k: v for k, v in _L0_ffn_all.items() if k in ('gate_w', 'up_w', 'down_w')}
    del _L0_ffn_all
    return {'x': x, 'ctx_1024': ctx_1024, 'L0_xattn_Wq': _L0_xattn_in['Wq'], 'L0_xattn_bq': _L0_xattn_in['bq'], 'L0_xattn_Wk': _L0_xattn_in['Wk'], 'L0_xattn_bk': _L0_xattn_in['bk'], 'L0_ffn_gate_w': _L0_ffn_in['gate_w'], 'L0_ffn_up_w': _L0_ffn_in['up_w'], 'L0_ffn_down_w': _L0_ffn_in['down_w']}

def reference(x, ctx_1024, L0_xattn_Wq, L0_xattn_bq, L0_xattn_Wk, L0_xattn_bk, L0_ffn_gate_w, L0_ffn_up_w, L0_ffn_down_w):
    import jax
    import jax.numpy as jnp

    def _L0_xattn_ref(teacher_logits, teacher_features, Wq, bq, Wk, bk):
        import jax, jax.numpy as jnp
        import numpy as np
        query = jnp.einsum('bnc,dc->bnd', teacher_features, Wq) + bq
        key = jnp.einsum('bnc,dc->bnd', teacher_features, Wk) + bk
        energy = jnp.einsum('bnd,bmd->bnm', query, key)
        attention = jax.nn.softmax(energy, axis=-1)
        x_m = jnp.einsum('bln,bmn->blm', teacher_logits, attention)
        return x_m

    def _L0_ffn_ref(x, gate_w, up_w, down_w):
        import jax, jax.numpy as jnp
        import numpy as np
        _FP8_MAX = 448.0
        _BLOCK = 32
        _EPS = 1e-30

        def _mx_dequant(t):
            rows, feat = t.shape
            blocks = t.reshape(rows, feat // _BLOCK, _BLOCK)
            max_abs = jnp.max(jnp.abs(blocks), axis=-1)
            scales = jnp.maximum(max_abs / _FP8_MAX, _EPS)
            q = (blocks / scales[..., None]).astype(jnp.float8_e4m3fn).astype(jnp.float32)
            return (q * scales[..., None]).reshape(rows, feat)

        def _mx_linear(x2d, w):
            return _mx_dequant(x2d) @ _mx_dequant(w).T
        B, S, H = x.shape
        x2d = x.reshape(B * S, H)
        gate = _mx_linear(x2d, gate_w)
        up = _mx_linear(x2d, up_w)
        h = jax.nn.silu(gate) * up
        out = _mx_linear(h, down_w)
        return out.reshape(B, S, H)
    x = x + _L0_xattn_ref(_layernorm(x, axis=-1), ctx_1024, L0_xattn_Wq, L0_xattn_bq, L0_xattn_Wk, L0_xattn_bk)
    x = x + _L0_ffn_ref(_layernorm(x, axis=-1), L0_ffn_gate_w, L0_ffn_up_w, L0_ffn_down_w)
    return x

_drawn_inputs = setup_inputs


def setup_inputs(seed=0):
    import zlib

    import numpy as np

    out = dict(_drawn_inputs(seed))
    spreads = {'L0_xattn_bq': (0.0, 0.1), 'L0_xattn_bk': (0.0, 0.1)}
    factors = {}
    for name, (base, spread) in spreads.items():
        noise = np.random.default_rng([zlib.crc32(name.encode()), seed]).standard_normal(out[name].shape)
        drawn = base * np.exp(spread * noise) if base else spread * noise
        out[name] = jnp.asarray(drawn.astype(out[name].dtype))
    for name, factor in factors.items():
        out[name] = (out[name] * factor).astype(out[name].dtype)
    return out
```

```python
from contextlib import ExitStack

import concourse.bass as bass
from concourse import mybir

F32 = mybir.dt.float32
BF16 = mybir.dt.bfloat16
F16 = mybir.dt.float16
I32 = mybir.dt.int32
ALU = mybir.AluOpType
ACT = mybir.ActivationFunctionType
AX = mybir.AxisListType

P = 128
BLOCK = 32
FP8_MAX = 448.0
TINY = 1e-30
LN_EPS = 1e-5
MAGIC = float(2 ** 20)
MAGIC_FLOOR = 1.5 * 2 ** 14
EXPONENT_BITS = 0x7F800000
X_SCALE = float(2 ** 10)
ROOM = 64.0
STAGE1_STEPS = 26
SLOT_STEPS = 15


def xattn_ffn(nc, x, ctxT, wqT, bq, wkT, bk, gate_w, up_w, down_w, ident, out):
    B, L, H = x.shape
    C = ctxT.shape[1]
    I = gate_w.shape[0]
    LT = L // P
    HT = H // P
    CT = C // P
    IT = I // P
    CH = I // 512
    RT = B * LT
    UNIT = 2048
    GROUPS = UNIT // 512
    assert L == H == 512 and C % P == 0 and CH == B and HT == B and IT == 4 * GROUPS

    x_rows = x.rearrange("b (t p) h -> b p t h", p=P)
    out_rows = out.rearrange("b (t p) h -> (b t) p h", p=P)
    ctx_cols = ctxT.rearrange("b (t p) n -> b p t n", p=P)
    gate_rows = gate_w.rearrange("(c t p) h -> c p t h", p=P, t=4)
    up_rows = up_w.rearrange("(c t p) h -> c p t h", p=P, t=4)
    down_rows = down_w.rearrange("(c p) i -> c p i", p=P)

    with ExitStack() as stack:
        def sb(name, shape, dt):
            return stack.enter_context(nc.sbuf_tensor(name, shape, dt))

        def bank(name):
            return stack.enter_context(nc.psum_tensor(name, [P, 512], F32))

        def sem(name):
            return stack.enter_context(nc.semaphore(name))

        X = sb("X", [P, RT, H], F32)
        gu_hi = sb("gu_hi", [P, HT, 2, CH, 512], F16)
        gu_lo = sb("gu_lo", [P, HT, 2, CH, 512], F16)
        dn_hi = sb("dn_hi", [P, IT, H], F16)
        dn_lo = sb("dn_lo", [P, IT, H], F16)
        W = [sb(f"W{k}", [P, UNIT], F32) for k in range(3)]
        absW = sb("absW", [P, UNIT], BF16)
        AT = sb("AT", [P, HT, 512], F32)
        XT = sb("XT", [P, HT, 512], F32)
        probs = sb("probs", [P, LT, 512], F32)
        ctx_sb = sb("ctx_sb", [P, CT, 512], F32)
        qT = sb("qT", [P, 512], F32)
        kT = sb("kT", [P, 512], F32)
        xn = sb("xn", [P, 2, H], F32)
        wq_sb = sb("wq_sb", [P, CT, P], F32)
        wk_sb = sb("wk_sb", [P, CT, P], F32)
        bq_sb = sb("bq_sb", [P, 1], F32)
        bk_sb = sb("bk_sb", [P, 1], F32)
        idf = sb("idf", [P, P], F32)
        neg_id = sb("neg_id", [P, P], F16)
        NB = UNIT // BLOCK
        amax = sb("amax", [P, NB], F32)
        scale = sb("scale", [P, 3, NB], F32)
        rscale = sb("rscale", [P, NB], F32)
        dscale = sb("dscale", [P, NB], F32)
        smax = sb("smax", [P, 3], F32)
        umax = sb("umax", [P, 3], F32)
        pow2 = sb("pow2", [P, 1], F32)
        rpow2 = sb("rpow2", [P, 1], F32)
        unscale = sb("unscale", [P, 3, 4], F32)
        stats = sb("stats", [P, LT, 6], F32)
        mv = sb("mv", [P, LT, 2], F32)
        veps = sb("veps", [P, LT], F32)
        rstd = sb("rstd", [P, LT], F32)
        nmean = sb("nmean", [P, LT], F32)
        nmr = sb("nmr", [P, LT], F32)
        mhalf = sb("mhalf", [P, LT], F32)
        pool_idle = sb("pool_idle", [P, 4], F32)
        dve_idle = sb("dve_idle", [P, 1], F32)
        nmax = sb("nmax", [P, LT], F32)
        esum = sb("esum", [P, LT], F32)
        rsum = sb("rsum", [P, LT], F32)
        xstats = sb("xstats", [P, 6], F32)
        xmv = sb("xmv", [P, 2], F32)
        XB = H // BLOCK
        xamax = sb("xamax", [P, XB], F32)
        xscale = sb("xscale", [P, XB], F32)
        xrscale = sb("xrscale", [P, XB], F32)
        xdscale = sb("xdscale", [P, XB], F32)
        hpow2 = sb("hpow2", [P, 1], F32)
        odown = sb("odown", [P, 4], F32)
        h = W[0]
        hw = W[1]
        silu = probs
        hT_hi = AT[:, 0:2, :].bitcast(F16).rearrange("p a n -> p (a n)")
        hT_lo = AT[:, 2:4, :].bitcast(F16).rearrange("p a n -> p (a n)")
        xT_hi = XT[:, 0, :].bitcast(F16)[:, 0:512]
        xT_lo = XT[:, 0, :].bitcast(F16)[:, 512:1024]
        xw = XT[:, 1, :]
        absX = XT[:, 2, :].bitcast(BF16)[:, 0:512]

        G = [bank(f"G{i}") for i in range(4)]
        TB = [bank(f"TB{i}") for i in range(2)]
        AB = [bank(f"AB{i}") for i in range(2)]

        consts_in = sem("consts_in")
        x_in = sem("x_in")
        ctx_in = sem("ctx_in")
        w_in = [sem(f"w_in{k}") for k in range(3)]
        out_written = sem("out_written")
        dve_step = sem("dve_step")
        pool_step = sem("pool_step")
        const_ready = sem("const_ready")
        stats_ready = sem("stats_ready")
        rstd_ready = sem("rstd_ready")
        xn_ready = sem("xn_ready")
        att_ready = sem("att_ready")
        att_taken = sem("att_taken")
        energy_ready = sem("energy_ready")
        nmax_ready = sem("nmax_ready")
        exp_ready = sem("exp_ready")
        probs_ready = sem("probs_ready")
        xm_ready = sem("xm_ready")
        g_free = sem("g_free")
        smax_ready = sem("smax_ready")
        umax_ready = sem("umax_ready")
        wv_ready = sem("wv_ready")
        wabs_ready = sem("wabs_ready")
        wabs_used = sem("wabs_used")
        wd_ready = sem("wd_ready")
        turned = sem("turned")
        hi_ready = sem("hi_ready")
        rest_ready = sem("rest_ready")
        lo_ready = sem("lo_ready")
        xs_ready = sem("xs_ready")
        xr_ready = sem("xr_ready")
        xnorm_ready = sem("xnorm_ready")
        xv_ready = sem("xv_ready")
        xabs_ready = sem("xabs_ready")
        xd_ready = sem("xd_ready")
        x_turned = sem("x_turned")
        xhi_ready = sem("xhi_ready")
        xrest_ready = sem("xrest_ready")
        xlo_ready = sem("xlo_ready")
        gate_ready = sem("gate_ready")
        up_ready = sem("up_ready")
        silu_ready = sem("silu_ready")
        h_ready = sem("h_ready")
        hv_ready = sem("hv_ready")
        habs_ready = sem("habs_ready")
        hd_ready = sem("hd_ready")
        down_ready = sem("down_ready")
        down_taken = sem("down_taken")

        class Steps:

            def __init__(self, s):
                self.s, self.base, self.n, self.turn, self.each = s, 0, 0, 0, 0

            def done(self, instruction):
                instruction.then_inc(self.s, 1)
                self.n += 1

            @property
            def value(self):
                return self.turn * self.each + (self.base + self.n)

            def enter(self, turn, each):
                self.base, self.n, self.turn, self.each = self.base + self.n, 0, turn, each

            def leave(self, turns):
                assert self.n == self.each, (self.n, self.each)
                self.base, self.n, self.turn, self.each = self.base + turns * self.each, 0, 0, 0

        UNITS = 3 * B
        LAST = RT - 1

        def slots(eng, slot):
            slot(-1, gu=False, hidden=False, result=False)
            slot(0, hidden=False, result=False)
            slot(1, result=False)
            yield
            slot(LAST, rows=False)
            slot(LAST + 1, gu=False, rows=False)
            slot(LAST + 2, gu=False, rows=False, hidden=False)

        def unit_part(gu, dn, k, g, b):
            if k < 2:
                return gu[:, g, k, b, :]
            return dn[:, 4 * g:4 * g + 4, bass.ds(b * P, P)]

        block = stack.enter_context(nc.Block())

        @block.sync
        def _(sp):
            def loads(b, first):
                if not first:
                    sp.wait_ge(att_ready, 10 * b - 8)
                sp.dma_start(ctx_sb[:, :, :], ctx_cols[b]).then_inc(ctx_in, 16)
                if not first:
                    sp.wait_ge(stats_ready, b)
                sp.dma_start(X[:, bass.ds(b * LT, LT), :], x_rows[b]).then_inc(x_in, 16)
                for k, rows in enumerate((gate_rows, up_rows, down_rows)):
                    if not first:
                        sp.wait_ge(turned, 12 * b - 12 + 4 * k + 4)
                    dst = W[k][:, :] if k == 2 else W[k][:, :].rearrange("p (t n) -> p t n", n=H)
                    sp.dma_start(dst, rows[b]).then_inc(w_in[k], 16)

            for dst, src in ((wq_sb[:, :, :], wqT.rearrange("(t p) d -> p t d", p=P)),
                             (wk_sb[:, :, :], wkT.rearrange("(t p) d -> p t d", p=P)),
                             (bq_sb[:, :], bq), (bk_sb[:, :], bk), (idf[:, :], ident)):
                sp.dma_start(dst, src).then_inc(consts_in, 16)
            loads(0, True)
            with sp.Fori(1, B) as b:
                loads(b, False)
            with sp.Fori(0, RT) as r:
                sp.wait_ge(down_taken, r + 2)
                sp.dma_start(out_rows[r], X[:, r, :]).then_inc(out_written, 16)
            sp.wait_ge(out_written, 16 * RT)

        @block.gpsimd
        def _(pool):
            own = Steps(pool_step)

            def carry_wait(n):
                nc.gpsimd.tensor_tensor(pool_idle[:, n:n + 1], mhalf[:, 0:1], mhalf[:, 0:1], ALU.mult)

            def inverse_std(m, n, ready):
                own.done(nc.gpsimd.tensor_scalar(veps[:, 0:n], m[:, :, 1], LN_EPS, 1.0, ALU.add, ALU.mult))
                own.done(nc.gpsimd.tensor_scalar(nmean[:, 0:n], m[:, :, 0], -1.0, 0.0, ALU.mult, ALU.add))
                pool.wait_ge(pool_step, own.value)
                own.done(nc.gpsimd.tensor_tensor(rstd[:, 0:n], veps[:, 0:n], mhalf[:, 0:n], ALU.pow))
                pool.wait_ge(pool_step, own.value)
                nc.gpsimd.tensor_tensor(nmr[:, 0:n], nmean[:, 0:n], rstd[:, 0:n], ALU.mult).then_inc(ready, 1)

            own.done(nc.gpsimd.memset(mhalf[:, :], -0.5))
            pool.wait_ge(pool_step, own.value)
            with pool.Fori(0, B) as b:
                own.enter(b, 3)
                pool.wait_ge(stats_ready, b + 1)
                carry_wait(0)
                inverse_std(mv, LT, rstd_ready)
                for k in range(3):
                    pool.wait_ge(smax_ready, 3 * b + (k + 1))
                    carry_wait(1 + k)
                    nc.gpsimd.partition_all_reduce(umax[:, k:k + 1], smax[:, k:k + 1], P,
                                                   bass.bass_isa.ReduceOp.max).then_inc(umax_ready, 1)
                own.leave(B)
            with pool.Fori(0, RT) as r:
                own.enter(r, 3)
                pool.wait_ge(xs_ready, r + 1)
                carry_wait(0)
                inverse_std(xmv[:, :].unsqueeze(1), 1, xr_ready)
                own.leave(RT)

        @block.tensor
        def _(pe):
            def turn4(dst, tiles):
                for j, t in enumerate(tiles):
                    last = pe.matmul(dst[:, j * P:(j + 1) * P], t, idf[:, :], is_transpose=True,
                                     start=(j == 0), stop=(j == 3))
                return last

            def turn_group(n, tiles):
                which, count = n
                pe.wait_ge(lo_ready, count + 1)
                turn4(TB[which], tiles).then_inc(turned, 1)

            def subtract_hi(n, hi):
                which, count = n
                pe.wait_ge(hi_ready, count + 1)
                pe.matmul(TB[which][:, :], neg_id[:, :], hi, start=False, stop=True,
                          skip_group_check=True).then_inc(rest_ready, 1)

            pe.wait_ge(consts_in, 80)
            pe.wait_ge(const_ready, 1)
            with pe.Fori(0, B) as b:
                def att_bank(i):
                    pe.wait_ge(att_taken, 10 * b + (i + 1))
                    return AB[i % 2]

                pe.wait_ge(ctx_in, 16 * b + 16)
                for i, w in enumerate((wq_sb, wk_sb)):
                    dst = att_bank(i)
                    for t in range(CT):
                        last = pe.matmul(dst[:, :], w[:, t, :], ctx_sb[:, t, :], start=(t == 0), stop=(t == CT - 1))
                    last.then_inc(att_ready, 1)
                for lt in range(LT):
                    dst = att_bank(2 + lt)
                    pe.wait_ge(xn_ready, LT * b + (lt + 1))
                    turn4(dst, [xn[:, lt % 2, j * P:(j + 1) * P] for j in range(HT)]).then_inc(att_ready, 1)
                pe.wait_ge(att_taken, 10 * b + 4)
                for nt in range(LT):
                    pe.wait_ge(g_free, LT * b + (nt + 1))
                    pe.matmul(G[nt][:, :], qT[:, nt * P:(nt + 1) * P], kT[:, :],
                              start=True, stop=True).then_inc(energy_ready, 1)

                def turn_unit(k):
                    pe.wait_ge(wd_ready, 3 * b + (k + 1))
                    for pair in range(GROUPS // 2):
                        for g in (2 * pair, 2 * pair + 1):
                            if k < 2:
                                tiles = [W[k][:, t * H + g * P:t * H + (g + 1) * P] for t in range(4)]
                            else:
                                tiles = [W[k][:, (4 * g + t) * P:(4 * g + t + 1) * P] for t in range(4)]
                            turn_group((g % 2, 12 * b + (4 * k + g)), tiles)
                        for g in (2 * pair, 2 * pair + 1):
                            subtract_hi((g % 2, 12 * b + (4 * k + g)), unit_part(gu_hi, dn_hi, k, g, b))

                turn_unit(0)
                for nt in range(LT):
                    dst = att_bank(6 + nt)
                    pe.wait_ge(probs_ready, LT * b + (nt + 1))
                    turn4(dst, [probs[:, nt, j * P:(j + 1) * P] for j in range(HT)]).then_inc(att_ready, 1)
                pe.wait_ge(att_taken, 10 * b + 12)
                for lt in range(LT):
                    for j in range(HT):
                        last = pe.matmul(G[lt][:, :], XT[:, j, lt * P:(lt + 1) * P], AT[:, j, :],
                                         start=(j == 0), stop=(j == HT - 1))
                    last.then_inc(xm_ready, 1)
                turn_unit(1)
                turn_unit(2)

            N0 = 4 * UNITS

            def slot(r, gu=True, rows=True, hidden=True, result=True):
                def products(c):
                    if not (isinstance(r, int) and r == 0 and c < 2):
                        pe.wait_ge(h_ready, 4 * r + (c - 1))
                    for g, ready in ((0, gate_ready), (1, up_ready)):
                        dst = G[2 * (c % 2) + g]
                        n = 0
                        for j in range(HT):
                            for a, w in ((xT_hi, gu_hi), (xT_hi, gu_lo), (xT_lo, gu_hi)):
                                last = pe.matmul(dst[:, :], a[:, j * P:(j + 1) * P], w[:, j, g, c, :],
                                                 start=(n == 0), stop=(n == 3 * HT - 1))
                                n += 1
                        last.then_inc(ready, 1)

                def group(g):
                    return g % 2, 4 * r + (N0 - 4 + g)

                def turn(g):
                    turn_group(group(g), [hw[:, (4 * g + t) * P:(4 * g + t + 1) * P] for t in range(4)])

                def rest(g):
                    subtract_hi(group(g), hT_hi[:, g * 512:(g + 1) * 512])

                def down(g):
                    for part in range(2):
                        if part == 1:
                            pe.wait_ge(lo_ready, group(g)[1] + 3)
                        for j in range(4 * g, 4 * g + 4):
                            for a, w in ((((hT_hi, dn_hi), (hT_hi, dn_lo)), ((hT_lo, dn_hi),))[part]):
                                last = pe.matmul(AB[0][:, :], a[:, j * P:(j + 1) * P], w[:, j, :],
                                                 start=(g == 0 and part == 0 and j == 0 and w is dn_hi),
                                                 stop=(g == 3 and part == 1 and j == IT - 1))
                    return last

                if gu:
                    pe.wait_ge(xlo_ready, r + 1)
                    for c in range(3):
                        products(c)
                if hidden:
                    pe.wait_ge(hd_ready, r)
                    turn(0)
                    turn(1)
                if gu:
                    products(3)
                if hidden:
                    rest(0)
                    rest(1)
                if rows:
                    pe.wait_ge(xd_ready, r + 2)
                    turn4(AB[1], [xw[:, j * P:(j + 1) * P] for j in range(HT)]).then_inc(x_turned, 1)
                if hidden:
                    pe.wait_ge(down_taken, r)
                    down(0)
                    turn(2)
                    turn(3)
                if rows:
                    pe.wait_ge(xhi_ready, r + 2)
                    pe.matmul(AB[1][:, :], neg_id[:, :], xT_hi, start=False, stop=True,
                              skip_group_check=True).then_inc(xrest_ready, 1)
                if hidden:
                    down(1)
                    rest(2)
                    rest(3)
                    down(2)
                    down(3).then_inc(down_ready, 1)

            plan = slots(pe, slot)
            next(plan)
            with pe.Fori(2, LAST) as r:
                slot(r)
            next(plan, None)

        @block.scalar
        def _(act):
            def take(dst, src, ready, count, signal, **kw):
                act.wait_ge(ready, count)
                nc.scalar.activation(dst, src, kw.pop("func", ACT.Copy), **kw).then_inc(signal, 1)

            act.wait_ge(consts_in, 80)
            act.sem_inc(att_taken, 2)
            act.sem_inc(lo_ready, 2)
            with act.Fori(0, B) as b:
                act.wait_ge(rstd_ready, b + 1)
                act.wait_ge(x_in, 16 * b + 16)
                def normalize(lt):
                    nc.scalar.activation(xn[:, lt % 2, :], X[:, b * LT + lt, :], ACT.Identity,
                                         scale=rstd[:, lt:lt + 1], bias=nmr[:, lt:lt + 1]).then_inc(xn_ready, 1)

                def take_rows(lt):
                    take(XT[:, :, lt * P:(lt + 1) * P], AB[lt % 2][:, :].rearrange("p (j n) -> p j n", n=P),
                         att_ready, 10 * b + (lt + 3), att_taken)

                normalize(0)
                normalize(1)
                for dst, bias, i in ((qT, bq_sb, 0), (kT, bk_sb, 1)):
                    take(dst[:, :], AB[i][:, :], att_ready, 10 * b + (i + 1), att_taken,
                         func=ACT.Identity, bias=bias[:, 0:1])
                take_rows(0)
                take_rows(1)
                normalize(2)
                normalize(3)
                take_rows(2)
                take_rows(3)

                def unit_abs(k):
                    act.wait_ge(wabs_used, 3 * b + (k + 1))
                    act.wait_ge(wv_ready, 3 * b + (k + 1))
                    nc.scalar.activation(absW[:, :], W[k][:, :], ACT.Abs, scale=MAGIC).then_inc(wabs_ready, 1)

                def unit_split(k):
                    for pair in range(GROUPS // 2):
                        for what, ready, signal in (((gu_hi, dn_hi), turned, hi_ready), ((gu_lo, dn_lo), rest_ready, lo_ready)):
                            for g in (2 * pair, 2 * pair + 1):
                                src = TB[g % 2][:, :]
                                if k == 2:
                                    src = src.rearrange("p (j n) -> p j n", n=P)
                                take(unit_part(*what, k, g, b), src, ready, 12 * b + (4 * k + g + 1), signal)

                unit_abs(0)
                for nt in range(LT):
                    act.wait_ge(nmax_ready, LT * b + (nt + 1))
                    nc.scalar.activation(probs[:, nt, :], G[nt][:, :], ACT.Exp, bias=nmax[:, nt:nt + 1],
                                         accum_out=esum[:, nt:nt + 1]).then_inc(exp_ready, 1)
                unit_abs(1)
                unit_split(0)
                for nt in range(LT):
                    take(AT[:, :, nt * P:(nt + 1) * P], AB[nt % 2][:, :].rearrange("p (j n) -> p j n", n=P),
                         att_ready, 10 * b + (nt + 7), att_taken)
                unit_abs(2)
                unit_split(1)
                unit_split(2)

            N0 = 4 * UNITS

            def slot(r, gu=True, rows=True, hidden=True, result=True):
                def silu_of(c):
                    act.wait_ge(gate_ready, 4 * r + (c + 1))
                    nc.scalar.activation(silu[:, c % 2, :], G[2 * (c % 2)][:, :], ACT.Silu,
                                         scale=unscale[:, 0, c:c + 1]).then_inc(silu_ready, 1)

                def part(dst, g, ready, signal):
                    take(dst[:, g * 512:(g + 1) * 512], TB[g % 2][:, :], ready, 4 * r + (N0 - 3 + g), signal)

                if hidden:
                    act.wait_ge(hv_ready, r)
                    nc.scalar.activation(absW[:, :], hw[:, :], ACT.Abs, scale=MAGIC).then_inc(habs_ready, 1)
                if gu:
                    silu_of(0)
                    silu_of(1)
                if rows:
                    act.wait_ge(xr_ready, r + 2)
                    nc.scalar.activation(xn[:, 0, :], X[:, r + 1, :], ACT.Identity,
                                         scale=rstd[:, 0:1], bias=nmr[:, 0:1]).then_inc(xnorm_ready, 1)
                if gu:
                    silu_of(2)
                if hidden:
                    part(hT_hi, 0, turned, hi_ready)
                    part(hT_hi, 1, turned, hi_ready)
                if rows:
                    act.wait_ge(xv_ready, r + 2)
                    nc.scalar.activation(absX, xw, ACT.Abs, scale=MAGIC).then_inc(xabs_ready, 1)
                if gu:
                    silu_of(3)
                if hidden:
                    part(hT_lo, 0, rest_ready, lo_ready)
                    part(hT_lo, 1, rest_ready, lo_ready)
                if rows:
                    take(xT_hi, AB[1][:, :], x_turned, r + 2, xhi_ready)
                if hidden:
                    part(hT_hi, 2, turned, hi_ready)
                    part(hT_hi, 3, turned, hi_ready)
                if rows:
                    take(xT_lo, AB[1][:, :], xrest_ready, r + 2, xlo_ready)
                if hidden:
                    part(hT_lo, 2, rest_ready, lo_ready)
                    part(hT_lo, 3, rest_ready, lo_ready)

            plan = slots(act, slot)
            next(plan)
            with act.Fori(2, LAST) as r:
                slot(r)
            next(plan, None)

        @block.vector
        def _(dve):
            own = Steps(dve_step)

            def carry_wait():
                dve.tensor_copy(dve_idle[:, :], bq_sb[:, :])

            def then(instruction):
                own.done(instruction)
                dve.wait_ge(dve_step, own.value)

            def blocks(t):
                return t.rearrange("p (b k) -> p b k", k=BLOCK)

            def each_block(s):
                return s.unsqueeze(2).broadcast_to([P, s.shape[1], BLOCK])

            def block_scales(src, am, sc):
                then(dve.tensor_reduce(am, blocks(src), AX.X, ALU.max, apply_absolute_value=True))
                then(dve.tensor_scalar(sc, am, 1.0 / FP8_MAX, TINY, ALU.mult, ALU.max))

            def round_e4m3(v, av, last=None):
                then(dve.scalar_tensor_tensor(v, av, MAGIC_FLOOR, v, ALU.max, ALU.add))
                then(dve.scalar_tensor_tensor(v, av, MAGIC_FLOOR, v, ALU.max, ALU.subtract))

            def power_of_two(p2, rp2, largest):
                then(dve.tensor_scalar(p2.bitcast(I32), largest.bitcast(I32), EXPONENT_BITS, None, ALU.bitwise_and))
                then(dve.reciprocal(rp2, p2))

            dve.wait_ge(consts_in, 80)
            dve.tensor_scalar(neg_id[:, :], idf[:, :], -1.0, None, ALU.mult).then_inc(const_ready, 1)
            dve.sem_inc(g_free, LT)
            dve.sem_inc(wabs_used, 1)
            dve.sem_inc(down_taken, 1)
            with dve.Fori(0, B) as b:
                own.enter(b, STAGE1_STEPS)
                dve.wait_ge(x_in, 16 * b + 16)
                for lt in range(LT):
                    last = dve.bn_stats(stats[:, lt, :], X[:, b * LT + lt, :])
                then(last)
                carry_wait()
                for lt in range(LT):
                    last = dve.bn_aggr(mv[:, lt, :], stats[:, lt, :])
                last.then_inc(stats_ready, 1)

                def unit_scale(k):
                    dve.wait_ge(w_in[k], 16 * b + 16)
                    block_scales(W[k][:, :], amax[:, :], scale[:, k, :])
                    dve.tensor_reduce(smax[:, k:k + 1], scale[:, k, :], AX.X, ALU.max).then_inc(smax_ready, 1)
                    then(dve.reciprocal(rscale[:, :], scale[:, k, :]))
                    dve.tensor_tensor(blocks(W[k][:, :]), blocks(W[k][:, :]), each_block(rscale[:, :]),
                                      ALU.mult).then_inc(wv_ready, 1)

                def unit_round(k):
                    dve.wait_ge(umax_ready, 3 * b + (k + 1))
                    power_of_two(pow2[:, :], rpow2[:, :], umax[:, k:k + 1])
                    dve.tensor_scalar(unscale[:, k, bass.ds(b, 1)], pow2[:, :], 1.0 / ROOM,
                                      1.0 / X_SCALE if k < 2 else 1.0, ALU.mult, ALU.mult)
                    then(dve.tensor_scalar(dscale[:, :], scale[:, k, :], rpow2[:, 0:1], -ROOM, ALU.mult, ALU.mult))
                    dve.wait_ge(wv_ready, 3 * b + (k + 1))
                    dve.wait_ge(wabs_ready, 3 * b + (k + 1))
                    then(dve.scalar_tensor_tensor(W[k][:, :], absW[:, :], MAGIC_FLOOR, W[k][:, :], ALU.max, ALU.add))
                    dve.scalar_tensor_tensor(W[k][:, :], absW[:, :], MAGIC_FLOOR, W[k][:, :], ALU.max,
                                             ALU.subtract).then_inc(wabs_used, 1)
                    dve.wait_ge(wabs_used, 3 * b + (k + 2))
                    dve.tensor_tensor(blocks(W[k][:, :]), blocks(W[k][:, :]), each_block(dscale[:, :]),
                                      ALU.mult).then_inc(wd_ready, 1)

                unit_scale(0)
                for nt in range(LT):
                    dve.wait_ge(energy_ready, LT * b + (nt + 1))
                    dve.tensor_reduce(nmax[:, nt:nt + 1], G[nt][:, :], AX.X, ALU.max, negate=True).then_inc(nmax_ready, 1)
                unit_scale(1)
                unit_round(0)
                for nt in range(LT):
                    dve.wait_ge(exp_ready, LT * b + (nt + 1))
                    then(dve.reciprocal(rsum[:, nt:nt + 1], esum[:, nt:nt + 1]))
                    dve.tensor_scalar(probs[:, nt, :], probs[:, nt, :], rsum[:, nt:nt + 1], None,
                                      ALU.mult).then_inc(probs_ready, 1)
                unit_scale(2)
                unit_round(1)
                for lt in range(LT):
                    dve.wait_ge(xm_ready, LT * b + (lt + 1))
                    dve.tensor_tensor(X[:, b * LT + lt, :], X[:, b * LT + lt, :], G[lt][:, :],
                                      ALU.add).then_inc(g_free, 1)
                unit_round(2)
                own.leave(B)

            def slot(r, gu=True, rows=True, hidden=True, result=True):
                def hidden_of(c):
                    dve.wait_ge(silu_ready, 4 * r + (c + 1))
                    dve.wait_ge(up_ready, 4 * r + (c + 1))
                    dve.scalar_tensor_tensor(h[:, c * 512:(c + 1) * 512], G[2 * (c % 2) + 1][:, :],
                                             unscale[:, 1, c:c + 1], silu[:, c % 2, :],
                                             ALU.mult, ALU.mult).then_inc(h_ready, 1)

                if result:
                    dve.wait_ge(down_ready, r - 1)
                    for n in range(HT):
                        cols = slice(n * P, (n + 1) * P)
                        last = dve.scalar_tensor_tensor(X[:, r - 2, cols], AB[0][:, cols], odown[:, n:n + 1],
                                                        X[:, r - 2, cols], ALU.mult, ALU.add)
                    last.then_inc(down_taken, 1)
                if hidden:
                    dve.wait_ge(habs_ready, r)
                    round_e4m3(hw[:, :], absW[:, :])
                    if result:
                        dve.wait_ge(down_taken, r)
                    then(dve.tensor_scalar(odown[:, :], unscale[:, 2, :], hpow2[:, 0:1], 1.0 / ROOM, ALU.mult, ALU.mult))
                    dve.tensor_tensor(blocks(hw[:, :]), blocks(hw[:, :]), each_block(dscale[:, :]),
                                      ALU.mult).then_inc(hd_ready, 1)
                if rows:
                    then(dve.bn_stats(xstats[:, :], X[:, r + 1, :]))
                    carry_wait()
                    dve.bn_aggr(xmv[:, :], xstats[:, :]).then_inc(xs_ready, 1)
                if gu:
                    hidden_of(0)
                    hidden_of(1)
                if rows:
                    dve.wait_ge(xnorm_ready, r + 2)
                    block_scales(xn[:, 0, :], xamax[:, :], xscale[:, :])
                    dve.tensor_scalar(xdscale[:, :], xscale[:, :], -X_SCALE, None, ALU.mult)
                    then(dve.reciprocal(xrscale[:, :], xscale[:, :]))
                    if not (isinstance(r, int) and r < 0):
                        dve.wait_ge(x_turned, r + 1)
                    dve.tensor_tensor(blocks(xw), blocks(xn[:, 0, :]), each_block(xrscale[:, :]),
                                      ALU.mult).then_inc(xv_ready, 1)
                if gu:
                    hidden_of(2)
                if rows:
                    dve.wait_ge(xabs_ready, r + 2)
                    round_e4m3(xw, absX)
                    dve.tensor_tensor(blocks(xw), blocks(xw), each_block(xdscale[:, :]), ALU.mult).then_inc(xd_ready, 1)
                if gu:
                    hidden_of(3)
                    dve.wait_ge(h_ready, 4 * r + 4)
                    block_scales(h[:, :], amax[:, :], scale[:, 0, :])
                    then(dve.tensor_reduce(smax[:, 0:1], scale[:, 0, :], AX.X, ALU.max))
                    power_of_two(hpow2[:, :], rpow2[:, :], smax[:, 0:1])
                    dve.tensor_scalar(dscale[:, :], scale[:, 0, :], rpow2[:, 0:1], -ROOM, ALU.mult, ALU.mult)
                    then(dve.reciprocal(rscale[:, :], scale[:, 0, :]))
                    if hidden:
                        dve.wait_ge(turned, 4 * r + 4 * UNITS)
                    dve.tensor_tensor(blocks(hw[:, :]), blocks(h[:, :]), each_block(rscale[:, :]),
                                      ALU.mult).then_inc(hv_ready, 1)

            plan = slots(dve, slot)
            next(plan)
            with dve.Fori(2, LAST) as r:
                own.enter(r - 2, SLOT_STEPS)
                slot(r)
                own.leave(LAST - 2)
            next(plan, None)




def kernel(x, ctx_1024, L0_xattn_Wq, L0_xattn_bq, L0_xattn_Wk, L0_xattn_bk, L0_ffn_gate_w, L0_ffn_up_w, L0_ffn_down_w):
    import numpy as np
    import concourse.bacc as bacc
    from concourse.bass_utils import run_bass_kernel_spmd

    arrays = {
        "x": np.ascontiguousarray(x),
        "ctxT": np.ascontiguousarray(np.transpose(ctx_1024, (0, 2, 1))),
        "wqT": np.ascontiguousarray(np.transpose(L0_xattn_Wq)),
        "bq": np.ascontiguousarray(np.reshape(L0_xattn_bq, (-1, 1))),
        "wkT": np.ascontiguousarray(np.transpose(L0_xattn_Wk)),
        "bk": np.ascontiguousarray(np.reshape(L0_xattn_bk, (-1, 1))),
        "gate_w": np.ascontiguousarray(L0_ffn_gate_w),
        "up_w": np.ascontiguousarray(L0_ffn_up_w),
        "down_w": np.ascontiguousarray(L0_ffn_down_w),
        "ident": np.eye(P, dtype=np.float32),
    }
    nc = bacc.Bacc("TRN2", target_bir_lowering=False, num_devices=1)
    args = [nc.dram_tensor(f"in_{n}", a.shape, mybir.dt.from_np(a.dtype), kind="ExternalInput").ap()
            for n, a in arrays.items()]
    out = nc.dram_tensor("out_y", arrays["x"].shape, F32, kind="ExternalOutput").ap()
    xattn_ffn(nc, *args, out)
    r = run_bass_kernel_spmd(nc, [{f"in_{n}": a for n, a in arrays.items()}], core_ids=[0])
    return r.results[0]["out_y"]
```

```python
from contextlib import ExitStack, contextmanager

import concourse.bass as bass
from concourse import mybir

F32 = mybir.dt.float32
BF16 = mybir.dt.bfloat16
F16 = mybir.dt.float16
I32 = mybir.dt.int32
ALU = mybir.AluOpType
ACT = mybir.ActivationFunctionType
AX = mybir.AxisListType

P = 128
BLOCK = 32
FP8_MAX = 448.0
TINY = 1e-30
LN_EPS = 1e-5
MAGIC = float(2 ** 20)
MAGIC_FLOOR = 1.5 * 2 ** 14
EXPONENT_BITS = 0x7F800000
X_SCALE = float(2 ** 10)
ROOM = 64.0
TURN_STEPS = 20
SLOT_STEPS = 15


def xattn_ffn(nc, x, ctxT, wqT, bq, wkT, bk, gate_w, up_w, down_w, ident, out):
    B, L, H = x.shape
    C = ctxT.shape[1]
    I = gate_w.shape[0]
    LT = L // P
    HT = H // P
    CT = C // P
    IT = I // P
    CH = I // 512
    RT = B * LT
    UNIT = 2048
    GROUPS = UNIT // 512
    RING = LT
    assert L == H == 512 and C % P == 0 and CH == B and HT == B and IT == 4 * GROUPS and RT > 2 * RING

    x_rows = x.rearrange("b (t p) h -> b p t h", p=P)
    out_rows = out.rearrange("b (t p) h -> (b t) p h", p=P)
    ctx_cols = ctxT.rearrange("b (t p) n -> b p t n", p=P)
    gate_rows = gate_w.rearrange("(c t p) h -> c p t h", p=P, t=4)
    up_rows = up_w.rearrange("(c t p) h -> c p t h", p=P, t=4)
    down_rows = down_w.rearrange("(c p) i -> c p i", p=P)
    x1_dram = nc.dram_tensor("x1_dram", (RT, P, H), F32, kind="Internal").ap()

    with ExitStack() as stack:
        def sb(name, shape, dt):
            return stack.enter_context(nc.sbuf_tensor(name, shape, dt))

        def bank(name):
            return stack.enter_context(nc.psum_tensor(name, [P, 512], F32))

        def sem(name):
            return stack.enter_context(nc.semaphore(name))

        gu_hi = sb("gu_hi", [P, HT, 2, CH, 512], F16)
        gu_lo = sb("gu_lo", [P, HT, 2, CH, 512], F16)
        dn_hi = sb("dn_hi", [P, IT, H], F16)
        dn_lo = sb("dn_lo", [P, IT, H], F16)
        X = sb("X", [P, LT, H], F32)
        h = sb("h", [P, RING, UNIT], F32)
        W = [sb(f"W{k}", [P, UNIT], F32) for k in range(3)]
        absW = sb("absW", [P, UNIT], BF16)
        AT = sb("AT", [P, HT, 512], F32)
        R1 = sb("R1", [P, 2, 512], F32)
        R2 = sb("R2", [P, 2, 512], F32)
        xT_hi = sb("xT_hi", [P, RING + 1, 512], F16)
        xT_lo = sb("xT_lo", [P, RING + 1, 512], F16)
        silu = sb("silu", [P, 2, 512], F32)
        wq_sb = sb("wq_sb", [P, CT, P], F32)
        wk_sb = sb("wk_sb", [P, CT, P], F32)
        bq_sb = sb("bq_sb", [P, 1], F32)
        bk_sb = sb("bk_sb", [P, 1], F32)
        idf = sb("idf", [P, P], F32)
        neg_id = sb("neg_id", [P, P], F16)
        NB = UNIT // BLOCK
        amax = sb("amax", [P, NB], F32)
        scale = sb("scale", [P, 3, NB], F32)
        rscale = sb("rscale", [P, NB], F32)
        dscale = sb("dscale", [P, NB], F32)
        smax = sb("smax", [P, 3], F32)
        umax = sb("umax", [P, 3], F32)
        pow2 = sb("pow2", [P, 1], F32)
        rpow2 = sb("rpow2", [P, 1], F32)
        unscale = sb("unscale", [P, 3, 4], F32)
        now_unscale = sb("now_unscale", [P, 2], F32)
        stats = sb("stats", [P, LT, 6], F32)
        mv = sb("mv", [P, LT, 2], F32)
        veps = sb("veps", [P, LT], F32)
        rstd = sb("rstd", [P, LT], F32)
        nmean = sb("nmean", [P, LT], F32)
        nmr = sb("nmr", [P, LT], F32)
        mhalf = sb("mhalf", [P, LT], F32)
        pool_idle = sb("pool_idle", [P, 4], F32)
        dve_idle = sb("dve_idle", [P, 1], F32)
        nmax = sb("nmax", [P, LT], F32)
        esum = sb("esum", [P, LT], F32)
        rsum = sb("rsum", [P, LT], F32)
        xstats = sb("xstats", [P, 6], F32)
        xmv = sb("xmv", [P, 2], F32)
        XB = H // BLOCK
        xamax = sb("xamax", [P, XB], F32)
        xscale = sb("xscale", [P, NB], F32)
        xrscale = sb("xrscale", [P, XB], F32)
        xdscale = sb("xdscale", [P, XB], F32)
        hpow2 = sb("hpow2", [P, 1], F32)
        hrpow2 = sb("hrpow2", [P, 1], F32)
        odown = sb("odown", [P, 1 + RING, HT], F32)
        ctx_sb = R1
        XT = R1
        qT, kT = R2[:, 0, :], R2[:, 1, :]
        xn = R2
        probs = h[:, :, 3 * 512:]
        rows0 = h[:, 0, :]
        hT_hi = AT[:, 0:2, :].bitcast(F16).rearrange("p a n -> p (a n)")
        hT_lo = AT[:, 2:4, :].bitcast(F16).rearrange("p a n -> p (a n)")
        xw = R2[:, 0, :]
        absX = R1[:, 0, :].bitcast(BF16)[:, 0:512]
        row_in, row_out = W[0][:, 0:H], X[:, 1, :]

        G = [bank(f"G{i}") for i in range(4)]
        TB = [bank(f"TB{i}") for i in range(2)]
        AB = [bank(f"AB{i}") for i in range(2)]

        consts_in = sem("consts_in")
        x_in = sem("x_in")
        ctx_in = sem("ctx_in")
        w_in = [sem(f"w_in{k}") for k in range(3)]
        x1_written = sem("x1_written")
        row_loaded = sem("row_loaded")
        residual_loaded = sem("residual_loaded")
        out_written = sem("out_written")
        dve_step = sem("dve_step")
        pool_step = sem("pool_step")
        const_ready = sem("const_ready")
        stats_ready = sem("stats_ready")
        rstd_ready = sem("rstd_ready")
        xn_ready = sem("xn_ready")
        att_ready = sem("att_ready")
        att_taken = sem("att_taken")
        energy_ready = sem("energy_ready")
        nmax_ready = sem("nmax_ready")
        exp_ready = sem("exp_ready")
        probs_ready = sem("probs_ready")
        xm_ready = sem("xm_ready")
        xm_taken = sem("xm_taken")
        rows0_ready = sem("rows0_ready")
        rows0_v = sem("rows0_v")
        rows0_abs = sem("rows0_abs")
        rows0_d = sem("rows0_d")
        smax_ready = sem("smax_ready")
        umax_ready = sem("umax_ready")
        wv_ready = sem("wv_ready")
        wabs_ready = sem("wabs_ready")
        wabs_used = sem("wabs_used")
        wd_ready = sem("wd_ready")
        turned = sem("turned")
        hi_ready = sem("hi_ready")
        rest_ready = sem("rest_ready")
        lo_ready = sem("lo_ready")
        xs_ready = sem("xs_ready")
        xr_ready = sem("xr_ready")
        xnorm_ready = sem("xnorm_ready")
        xv_ready = sem("xv_ready")
        xabs_ready = sem("xabs_ready")
        xd_ready = sem("xd_ready")
        x_turned = sem("x_turned")
        xhi_ready = sem("xhi_ready")
        xrest_ready = sem("xrest_ready")
        xlo_ready = sem("xlo_ready")
        gate_ready = sem("gate_ready")
        unscale_ready = sem("unscale_ready")
        up_ready = sem("up_ready")
        silu_ready = sem("silu_ready")
        h_ready = sem("h_ready")
        hv_ready = sem("hv_ready")
        habs_ready = sem("habs_ready")
        hd_ready = sem("hd_ready")
        down_ready = sem("down_ready")
        down_taken = sem("down_taken")

        class Steps:

            def __init__(self, s):
                self.s, self.base, self.n, self.turn, self.each = s, 0, 0, 0, 0

            def done(self, instruction):
                instruction.then_inc(self.s, 1)
                self.n += 1

            @property
            def value(self):
                return self.turn * self.each + (self.base + self.n)

            def enter(self, turn, each):
                self.base, self.n, self.turn, self.each = self.base + self.n, 0, turn, each

            def leave(self, turns):
                assert self.n == self.each, (self.n, self.each)
                self.base, self.n, self.turn, self.each = self.base + turns * self.each, 0, 0, 0

        ROWS0 = 2

        def unit(b, k):
            return (0, 1, 3)[k] if isinstance(b, int) and b == 0 else 3 * b + (k + 1)

        UNITS = 3 * B + 1

        def rows0_half(half):
            return (rows0[:, half * UNIT // 2:(half + 1) * UNIT // 2], slice(half * NB // 2, (half + 1) * NB // 2))

        def group(u, g):
            return g % 2, 4 * u + g

        def unit_part(gu, dn, k, g, b):
            if k < 2:
                return gu[:, g, k, b, :]
            return dn[:, 4 * g:4 * g + 4, bass.ds(b * P, P)]

        FIRST, LAST = RING, RT - 1

        def run_slots(slot, fori):
            slot(FIRST, result=False)
            with fori(FIRST + 1, LAST) as r:
                slot(r)
            slot(LAST, last=True)

        TAIL = RT - RING

        def hidden_rows(j):
            return W[(2, 0, 1, 2)[j - TAIL] if isinstance(j, int) and j >= TAIL else 1][:, :]

        def down_bank(j):
            return AB[(j - TAIL + 1) % 2 if isinstance(j, int) and j >= TAIL else 0]

        def odown_of(j):
            return odown[:, j - TAIL + 1 if isinstance(j, int) and j >= TAIL else 0, :]

        block = stack.enter_context(nc.Block())

        @block.sync
        def _(sp):
            def load_unit(b, k):
                rows = (gate_rows, up_rows, down_rows)[k]
                dst = W[k][:, :] if k == 2 else W[k][:, :].rearrange("p (t n) -> p t n", n=H)
                sp.dma_start(dst, rows[b]).then_inc(w_in[k], 16)

            def store_rows(b):
                sp.wait_ge(xm_taken, LT * b + LT)
                sp.dma_start(x1_dram[bass.ds(b * LT, LT)].rearrange("t p h -> p t h"), X[:, :, :]).then_inc(x1_written, 16)

            def loads(b):
                sp.wait_ge(turned, group(unit(b - 1, 0), 4)[1])
                load_unit(b, 0)
                sp.wait_ge(xm_ready, LT * b)
                sp.dma_start(ctx_sb[:, :, :], ctx_cols[b]).then_inc(ctx_in, 16)
                store_rows(b - 1)
                sp.wait_ge(turned, group(unit(b - 1, 1), 4)[1])
                load_unit(b, 1)
                sp.wait_ge(x1_written, 16 * b)
                if isinstance(b, int):
                    sp.wait_ge(rows0_ready, LT)
                sp.dma_start(X[:, :, :], x_rows[b]).then_inc(x_in, 16)
                sp.wait_ge(turned, group(unit(b - 1, 2), 4)[1])
                load_unit(b, 2)

            sp.dma_start(ctx_sb[:, :, :], ctx_cols[0]).then_inc(ctx_in, 16)
            load_unit(0, 0)
            for dst, src in ((wq_sb[:, :, :], wqT.rearrange("(t p) d -> p t d", p=P)),
                             (wk_sb[:, :, :], wkT.rearrange("(t p) d -> p t d", p=P)),
                             (bq_sb[:, :], bq), (bk_sb[:, :], bk), (idf[:, :], ident)):
                sp.dma_start(dst, src).then_inc(consts_in, 16)
            sp.dma_start(X[:, :, :], x_rows[0]).then_inc(x_in, 16)
            load_unit(0, 1)
            load_unit(0, 2)
            loads(1)
            with sp.Fori(2, B) as b:
                loads(b)
            sp.wait_ge(turned, group(unit(B - 1, 0), 4)[1])
            sp.dma_start(row_in, x1_dram[FIRST]).then_inc(row_loaded, 16)
            store_rows(B - 1)
            sp.wait_ge(x1_written, 16 * B)

            def load_row(r):
                sp.dma_start(row_in, x1_dram[r]).then_inc(row_loaded, 16)

            def load_residual(j):
                sp.dma_start(row_out, x1_dram[j]).then_inc(residual_loaded, 16)

            def store_out(j):
                sp.wait_ge(down_taken, j + 1)
                sp.dma_start(out_rows[j], row_out).then_inc(out_written, 16)
                sp.wait_ge(out_written, 16 * (j + 1))

            load_residual(0)
            def next_row(r):
                sp.wait_ge(xnorm_ready, r - FIRST)
                load_row(r)

            next_row(FIRST + 1)
            with sp.Fori(FIRST + 2, RT) as r:
                next_row(r)
                store_out(r - (FIRST + 2))
                load_residual(r - (FIRST + 1))
            with sp.Fori(RT - FIRST - 2, RT - 1) as j:
                store_out(j)
                load_residual(j + 1)
            store_out(RT - 1)

        @block.gpsimd
        def _(pool):
            own = Steps(pool_step)

            def carry_wait(n):
                nc.gpsimd.tensor_tensor(pool_idle[:, n:n + 1], mhalf[:, 0:1], mhalf[:, 0:1], ALU.mult)

            def inverse_std(m, n, ready):
                own.done(nc.gpsimd.tensor_scalar(veps[:, 0:n], m[:, :, 1], LN_EPS, 1.0, ALU.add, ALU.mult))
                own.done(nc.gpsimd.tensor_scalar(nmean[:, 0:n], m[:, :, 0], -1.0, 0.0, ALU.mult, ALU.add))
                pool.wait_ge(pool_step, own.value)
                own.done(nc.gpsimd.tensor_tensor(rstd[:, 0:n], veps[:, 0:n], mhalf[:, 0:n], ALU.pow))
                pool.wait_ge(pool_step, own.value)
                nc.gpsimd.tensor_tensor(nmr[:, 0:n], nmean[:, 0:n], rstd[:, 0:n], ALU.mult).then_inc(ready, 1)

            def unit_max(b, k):
                pool.wait_ge(smax_ready, 3 * b + (k + 1))
                carry_wait(1 + k)
                nc.gpsimd.partition_all_reduce(umax[:, k:k + 1], smax[:, k:k + 1], P,
                                               bass.bass_isa.ReduceOp.max).then_inc(umax_ready, 1)

            own.done(nc.gpsimd.memset(mhalf[:, :], -0.5))
            pool.wait_ge(pool_step, own.value)
            unit_max(0, 0)
            pool.wait_ge(stats_ready, 1)
            inverse_std(mv, LT, rstd_ready)
            unit_max(0, 1)
            pool.wait_ge(stats_ready, 2)
            inverse_std(mv, LT, rstd_ready)
            unit_max(0, 2)
            with pool.Fori(1, B) as b:
                own.enter(b - 1, 3)
                unit_max(b, 0)
                pool.wait_ge(stats_ready, b + 2)
                carry_wait(0)
                inverse_std(mv, LT, rstd_ready)
                unit_max(b, 1)
                unit_max(b, 2)
                own.leave(B - 1)
            with pool.Fori(0, RT - FIRST) as n:
                own.enter(n, 3)
                pool.wait_ge(xs_ready, n + 1)
                carry_wait(0)
                inverse_std(xmv[:, :].unsqueeze(1), 1, xr_ready)
                own.leave(RT - FIRST)

        @block.tensor
        def _(pe):
            def turn4(dst, tiles):
                for j, t in enumerate(tiles):
                    last = pe.matmul(dst[:, j * P:(j + 1) * P], t, idf[:, :], is_transpose=True,
                                     start=(j == 0), stop=(j == 3))
                return last

            def turn_group(u, g, tiles):
                which, n = group(u, g)
                if not isinstance(n, int) or n >= 2:
                    pe.wait_ge(lo_ready, n - 1)
                turn4(TB[which], tiles).then_inc(turned, 1)

            def subtract_hi(u, g, hi):
                which, n = group(u, g)
                pe.wait_ge(hi_ready, n + 1)
                pe.matmul(TB[which][:, :], neg_id[:, :], hi, start=False, stop=True,
                          skip_group_check=True).then_inc(rest_ready, 1)

            def half_products(n, g, tile, chunk):
                dst = G[2 * n[0] + g]
                m = 0
                for j in range(HT):
                    for a, w in ((xT_hi, gu_hi), (xT_hi, gu_lo), (xT_lo, gu_hi)):
                        last = pe.matmul(dst[:, :], a[:, tile, j * P:(j + 1) * P], w[:, j, g, chunk, :],
                                         start=(m == 0), stop=(m == 3 * HT - 1))
                        m += 1
                last.then_inc((gate_ready, up_ready)[g], 1)

            def turn_unit(b, k):
                u = unit(b, k)
                pe.wait_ge(wd_ready, u + 1)
                for pair in range(GROUPS // 2):
                    for g in (2 * pair, 2 * pair + 1):
                        if k < 2:
                            tiles = [W[k][:, t * H + g * P:t * H + (g + 1) * P] for t in range(4)]
                        else:
                            tiles = [W[k][:, (4 * g + t) * P:(4 * g + t + 1) * P] for t in range(4)]
                        turn_group(u, g, tiles)
                    yield
                    for g in (2 * pair, 2 * pair + 1):
                        subtract_hi(u, g, unit_part(gu_hi, dn_hi, k, g, b))
                    yield

            def turn(b, attention=True, products=True):
                taken = 14 * b
                nothing = iter(())

                def half(r, g):
                    if products:
                        if r == 0 and g == 0:
                            pe.wait_ge(lo_ready, group(3 * b - 1, 4)[1])
                        if g == 0:
                            pe.wait_ge(h_ready, LT * b + (r - LT + 1))
                        half_products((r % 2,), g, r, b - 1)

                def attend(step, *args):
                    if attention:
                        step(*args)

                def project(i):
                    w = (wq_sb, wk_sb)[i]
                    pe.wait_ge(ctx_in, 16 * b + 16)
                    if not isinstance(b, int):
                        pe.wait_ge(xm_taken, LT * b + (i - 1))
                    for t in range(CT):
                        last = pe.matmul(AB[i][:, :], w[:, t, :], ctx_sb[:, t, :], start=(t == 0), stop=(t == CT - 1))
                    last.then_inc(att_ready, 1)

                def energies(nt):
                    pe.wait_ge(att_taken, taken + max(nt + 1, 2))
                    pe.matmul(AB[nt % 2][:, :], qT[:, nt * P:(nt + 1) * P], kT,
                              start=True, stop=True).then_inc(energy_ready, 1)

                def turn_probs(nt):
                    pe.wait_ge(att_taken, taken + (nt + 7))
                    pe.wait_ge(probs_ready, LT * b + (nt + 1))
                    turn4(AB[nt % 2], [probs[:, nt, j * P:(j + 1) * P] for j in range(HT)]).then_inc(att_ready, 1)

                def turn_rows(lt):
                    if lt < 2:
                        pe.wait_ge(att_taken, taken + (lt + 5))
                    else:
                        pe.wait_ge(xm_taken, LT * b + (lt - 1))
                    pe.wait_ge(xn_ready, LT * b + (lt + 1))
                    turn4(AB[lt % 2], [xn[:, lt % 2, j * P:(j + 1) * P] for j in range(HT)]).then_inc(att_ready, 1)

                def attend_rows(lt, tiles=range(HT)):
                    if tiles[0] == 0:
                        pe.wait_ge(att_taken, taken + max(lt + 11, 12))
                    for j in tiles:
                        last = pe.matmul(AB[lt % 2][:, :], XT[:, lt % 2, j * P:(j + 1) * P], AT[:, j, :],
                                         start=(j == 0), stop=(j == HT - 1))
                    if tiles[-1] == HT - 1:
                        last.then_inc(xm_ready, 1)

                down = turn_unit(b - 1, 2) if products else nothing
                gate, up = (turn_unit(b, 0), turn_unit(b, 1)) if attention else (nothing, nothing)
                half(0, 0)
                attend(project, 0)
                attend(project, 1)
                half(0, 1)
                attend(energies, 0)
                attend(energies, 1)
                half(1, 0)
                next(down, None)
                half(1, 1)
                next(down, None)
                attend(energies, 2)
                attend(energies, 3)
                half(2, 0)
                next(down, None)
                attend(turn_rows, 0)
                attend(turn_rows, 1)
                next(down, None)
                half(2, 1)
                attend(turn_probs, 0)
                attend(turn_probs, 1)
                if products:
                    next(gate, None)
                attend(turn_probs, 2)
                attend(turn_probs, 3)
                if products:
                    next(gate, None)
                attend(attend_rows, 0)
                next(gate, None)
                attend(attend_rows, 1)
                next(gate, None)
                attend(turn_rows, 2)
                attend(turn_rows, 3)
                if not products:
                    next(gate)
                if not attention:
                    pe.wait_ge(xm_taken, RT)
                    turn_row(FIRST)
                half(3, 0)
                if products:
                    next(up, None)
                attend(attend_rows, 2)
                if products:
                    next(up, None)
                attend(attend_rows, 3, range(HT // 2))
                if products:
                    next(up, None)
                attend(attend_rows, 3, range(HT // 2, HT))
                if products:
                    next(up, None)
                if not attention:
                    subtract_row_hi(FIRST)
                half(3, 1)
                for part in (gate, up):
                    for _ in part:
                        pass

            pe.wait_ge(consts_in, 80)
            pe.wait_ge(const_ready, 1)
            turn(0, products=False)
            for pair, (done, count) in enumerate(((rows0_d, 1), (wd_ready, ROWS0 + 1))):
                pe.wait_ge(done, count)
                for t in (2 * pair, 2 * pair + 1):
                    turn_group(ROWS0, t, [rows0[:, t * H + j * P:t * H + (j + 1) * P] for j in range(HT)])
                for t in (2 * pair, 2 * pair + 1):
                    subtract_hi(ROWS0, t, xT_hi[:, t, :])
            with pe.Fori(1, B) as b:
                turn(b)

            def turn_row(r):
                pe.wait_ge(xd_ready, r - (FIRST - 1))
                turn4(AB[1], [xw[:, j * P:(j + 1) * P] for j in range(HT)]).then_inc(x_turned, 1)

            def subtract_row_hi(r):
                pe.wait_ge(xhi_ready, r - (FIRST - 1))
                pe.matmul(AB[1][:, :], neg_id[:, :], xT_hi[:, RING, :], start=False, stop=True,
                          skip_group_check=True).then_inc(xrest_ready, 1)

            turn(B, attention=False)

            def turn_hidden(j, g):
                hw = hidden_rows(j)
                turn_group(j + UNITS, g, [hw[:, (4 * g + t) * P:(4 * g + t + 1) * P] for t in range(4)])

            def rest(j, g):
                subtract_hi(j + UNITS, g, hT_hi[:, g * 512:(g + 1) * 512])

            def down_part(j, g, part):
                if part == 1:
                    pe.wait_ge(lo_ready, group(j + UNITS, g)[1] + 1)
                for k in range(4 * g, 4 * g + 4):
                    for a, w in ((((hT_hi, dn_hi), (hT_hi, dn_lo)), ((hT_lo, dn_hi),))[part]):
                        last = pe.matmul(down_bank(j)[:, :], a[:, k * P:(k + 1) * P], w[:, k, :],
                                         start=(g == 0 and part == 0 and k == 0 and w is dn_hi),
                                         stop=(g == 3 and part == 1 and k == IT - 1))
                if g == 3 and part == 1:
                    last.then_inc(down_ready, 1)

            def slot(r, result=True, last=False):
                j = r - RING

                def products(c):
                    pe.wait_ge(h_ready, 4 * r + (c + 1))
                    half_products((c % 2,), 0, RING, c)
                    half_products((c % 2,), 1, RING, c)

                def down(g):
                    down_part(j, g, 0)
                    down_part(j, g, 1)

                pe.wait_ge(xlo_ready, r - (FIRST - 1))
                for c in range(3):
                    products(c)
                pe.wait_ge(hd_ready, r - (RING - 1))
                turn_hidden(j, 0)
                turn_hidden(j, 1)
                products(3)
                rest(j, 0)
                rest(j, 1)
                if not last:
                    turn_row(r + 1)
                if result:
                    pe.wait_ge(down_taken, r - RING)
                down(0)
                turn_hidden(j, 2)
                turn_hidden(j, 3)
                if not last:
                    subtract_row_hi(r + 1)
                down(1)
                rest(j, 2)
                rest(j, 3)
                down(2)
                down(3)

            run_slots(slot, pe.Fori)
            groups = [(j, g) for j in range(TAIL, RT) for g in range(GROUPS)]
            for n, (j, g) in enumerate(groups):
                if n == 0:
                    pe.wait_ge(hd_ready, j + 1)
                    turn_hidden(j, g)
                    rest(j, g)
                if g == 0 and j > TAIL:
                    pe.wait_ge(down_taken, j - 1)
                down_part(j, g, 0)
                if n + 1 < len(groups):
                    following = groups[n + 1]
                    if following[1] == 0:
                        pe.wait_ge(hd_ready, following[0] + 1)
                    turn_hidden(*following)
                down_part(j, g, 1)
                if n + 1 < len(groups):
                    rest(*following)

        @block.scalar
        def _(act):
            def take(dst, src, ready, count, signal, func=ACT.Copy, **kw):
                act.wait_ge(ready, count)
                nc.scalar.activation(dst, src, func, **kw).then_inc(signal, 1)

            def split_unit(u, dst, as_tiles=False, at_once=2):
                for first in range(0, GROUPS, at_once):
                    for part, ready, signal in ((0, turned, hi_ready), (1, rest_ready, lo_ready)):
                        for g in range(first, first + at_once):
                            which, n = group(u, g)
                            src = TB[which][:, :]
                            if as_tiles:
                                src = src.rearrange("p (j n) -> p j n", n=P)
                            take(dst(part, g), src, ready, n + 1, signal)
                        yield

            def split_weight(b, k):
                return split_unit(unit(b, k), lambda part, g: unit_part(*((gu_hi, dn_hi), (gu_lo, dn_lo))[part], k, g, b),
                                  as_tiles=(k == 2))

            def unit_abs(u, v):
                if not isinstance(u, int) or u > 0:
                    act.wait_ge(wabs_used, u)
                act.wait_ge(wv_ready, u + 1)
                nc.scalar.activation(absW[:, :], v, ACT.Abs, scale=MAGIC).then_inc(wabs_ready, 1)

            def silu_of(n, pair, factor):
                act.wait_ge(gate_ready, n + 1)
                nc.scalar.activation(silu[:, pair, :], G[2 * pair][:, :], ACT.Silu,
                                     scale=factor).then_inc(silu_ready, 1)

            def turn(b, attention=True, products=True):
                nothing = iter(())

                def silu_tile(r):
                    if products:
                        if r == 0:
                            act.wait_ge(unscale_ready, b)
                        silu_of(LT * b + (r - LT), r % 2, now_unscale[:, 0:1])

                def attend(step, *args):
                    if attention:
                        step(*args)

                def take_projection(i):
                    take((qT, kT)[i], AB[i][:, :], att_ready, 10 * b + (i + 1), att_taken,
                         func=ACT.Identity, bias=(bq_sb, bk_sb)[i][:, 0:1])

                def exponentials(nt):
                    act.wait_ge(nmax_ready, LT * b + (nt + 1))
                    nc.scalar.activation(probs[:, nt, :], AB[nt % 2][:, :], ACT.Exp, bias=nmax[:, nt:nt + 1],
                                         accum_out=esum[:, nt:nt + 1]).then_inc(att_taken, 1)

                def take_probs(nt):
                    take(AT[:, :, nt * P:(nt + 1) * P], AB[nt % 2][:, :].rearrange("p (j n) -> p j n", n=P),
                         att_ready, 10 * b + (nt + 5), att_taken)

                def normalize(lt):
                    if lt == 0:
                        act.wait_ge(rstd_ready, b + 1 if isinstance(b, int) and b == 0 else b + 2)
                    nc.scalar.activation(xn[:, lt % 2, :], X[:, lt, :], ACT.Identity,
                                         scale=rstd[:, lt:lt + 1], bias=nmr[:, lt:lt + 1]).then_inc(xn_ready, 1)

                def take_rows(lt):
                    take(XT[:, lt % 2, :], AB[lt % 2][:, :], att_ready, 10 * b + (lt + (3 if lt < 2 else 7)), att_taken)

                down = split_weight(b - 1, 2) if products else nothing
                gate, up = (split_weight(b, 0), split_weight(b, 1)) if attention else (nothing, nothing)
                def abs_of(k):
                    if attention:
                        unit_abs(unit(b, k), W[k][:, :])

                if not attention:
                    silu_tile(0)
                    normalize_row(FIRST)
                    next(down)
                    row_abs(FIRST)
                    next(down)
                    silu_tile(1)
                    next(down)
                    next(down)
                    silu_tile(2)
                    take_row(FIRST, 0)
                    take_row(FIRST, 1)
                    silu_tile(3)
                    return
                silu_tile(0)
                attend(take_projection, 0)
                attend(take_projection, 1)
                abs_of(0)
                next(down, None)
                attend(exponentials, 0)
                attend(exponentials, 1)
                next(down, None)
                attend(exponentials, 2)
                attend(exponentials, 3)
                attend(normalize, 0)
                attend(normalize, 1)
                next(down, None)
                attend(take_rows, 0)
                attend(take_rows, 1)
                next(down, None)
                attend(take_probs, 0)
                attend(take_probs, 1)
                if products:
                    next(gate, None)
                attend(take_probs, 2)
                attend(take_probs, 3)
                if products:
                    abs_of(1)
                    next(gate, None)
                    next(gate, None)
                    silu_tile(1)
                    silu_tile(2)
                attend(normalize, 2)
                attend(normalize, 3)
                if products:
                    next(gate, None)
                else:
                    next(gate)
                    next(gate)
                attend(take_rows, 2)
                attend(take_rows, 3)
                if products:
                    next(up, None)
                    abs_of(2)
                    next(up, None)
                    next(up, None)
                else:
                    next(gate)
                    abs_of(1)
                    next(gate)
                    normalize_rows0()
                    next(up)
                    next(up)
                    rows0_absolutes(0)
                silu_tile(3)
                for _ in up:
                    pass

            def normalize_rows0():
                act.wait_ge(rstd_ready, 2)
                for lt in range(LT):
                    nc.scalar.activation(rows0[:, lt * H:(lt + 1) * H], X[:, lt, :], ACT.Identity,
                                         scale=rstd[:, lt:lt + 1], bias=nmr[:, lt:lt + 1]).then_inc(rows0_ready, 1)

            def rows0_absolutes(half):
                ready, count, done = ((rows0_v, 1, rows0_abs), (wv_ready, ROWS0 + 1, wabs_ready))[half]
                act.wait_ge(wabs_used, ROWS0)
                act.wait_ge(ready, count)
                nc.scalar.activation(absW[:, half * UNIT // 2:(half + 1) * UNIT // 2], rows0_half(half)[0],
                                     ACT.Abs, scale=MAGIC).then_inc(done, 1)

            act.wait_ge(consts_in, 80)
            act.wait_ge(x_in, 16)
            turn(0, products=False)
            rows0_absolutes(1)
            for _ in split_unit(ROWS0, lambda part, t: (xT_hi, xT_lo)[part][:, t, :]):
                pass
            unit_abs(unit(0, 2), W[2][:, :])
            with act.Fori(1, B) as b:
                turn(b)

            def normalize_row(r):
                act.wait_ge(xr_ready, r - (FIRST - 1))
                nc.scalar.activation(xw, row_in, ACT.Identity,
                                     scale=rstd[:, 0:1], bias=nmr[:, 0:1]).then_inc(xnorm_ready, 1)

            def row_abs(r):
                act.wait_ge(xv_ready, r - (FIRST - 1))
                nc.scalar.activation(absX, xw, ACT.Abs, scale=MAGIC).then_inc(xabs_ready, 1)

            def take_row(r, part):
                dst, ready, signal = ((xT_hi, x_turned, xhi_ready), (xT_lo, xrest_ready, xlo_ready))[part]
                take(dst[:, RING, :], AB[1][:, :], ready, r - (FIRST - 1), signal)

            turn(B, attention=False)

            def hidden_abs(j):
                act.wait_ge(hv_ready, j + 1)
                nc.scalar.activation(absW[:, :], hidden_rows(j), ACT.Abs, scale=MAGIC).then_inc(habs_ready, 1)

            def split_hidden(j, each=False):
                return split_unit(j + UNITS, lambda part, g: (hT_hi, hT_lo)[part][:, g * 512:(g + 1) * 512],
                                  at_once=1 if each else 2)

            def slot(r, result=True, last=False):
                hidden_abs(r - RING)
                split = split_hidden(r - RING)
                silu_of(4 * r, 0, unscale[:, 0, 0:1])
                silu_of(4 * r + 1, 1, unscale[:, 0, 1:2])
                if not last:
                    normalize_row(r + 1)
                if last:
                    hidden_abs(TAIL)
                silu_of(4 * r + 2, 0, unscale[:, 0, 2:3])
                next(split)
                if not last:
                    row_abs(r + 1)
                silu_of(4 * r + 3, 1, unscale[:, 0, 3:4])
                next(split)
                if not last:
                    take_row(r + 1, 0)
                next(split)
                if not last:
                    take_row(r + 1, 1)
                next(split)

            run_slots(slot, act.Fori)
            for j in range(TAIL, RT):
                for step, _ in enumerate(split_hidden(j, each=True)):
                    if step == (0, 2, 2, -1)[j - TAIL]:
                        hidden_abs(j + 1)

        @block.vector
        def _(dve):
            own = Steps(dve_step)

            def carry_wait():
                dve.tensor_copy(dve_idle[:, :], bq_sb[:, :])

            def then(instruction):
                own.done(instruction)
                dve.wait_ge(dve_step, own.value)

            def blocks(t):
                return t.rearrange("p (b k) -> p b k", k=BLOCK)

            def each_block(s):
                return s.unsqueeze(2).broadcast_to([P, s.shape[1], BLOCK])

            def block_scales(src, am, sc):
                then(dve.tensor_reduce(am, blocks(src), AX.X, ALU.max, apply_absolute_value=True))
                then(dve.tensor_scalar(sc, am, 1.0 / FP8_MAX, TINY, ALU.mult, ALU.max))

            def power_of_two(p2, rp2, largest):
                then(dve.tensor_scalar(p2.bitcast(I32), largest.bitcast(I32), EXPONENT_BITS, None, ALU.bitwise_and))
                then(dve.reciprocal(rp2, p2))

            def round_e4m3(v, av, read=None):
                then(dve.scalar_tensor_tensor(v, av, MAGIC_FLOOR, v, ALU.max, ALU.add))
                last = dve.scalar_tensor_tensor(v, av, MAGIC_FLOOR, v, ALU.max, ALU.subtract)
                if read is None:
                    then(last)
                else:
                    last.then_inc(read[0], 1)
                    dve.wait_ge(*read)

            def row_stats(n):
                for lt in range(LT):
                    last = dve.bn_stats(stats[:, lt, :], X[:, lt, :])
                then(last)
                if not isinstance(n, int):
                    carry_wait()
                for lt in range(LT):
                    last = dve.bn_aggr(mv[:, lt, :], stats[:, lt, :])
                last.then_inc(stats_ready, 1)

            def unit_scale(b, k):
                dve.wait_ge(w_in[k], 16 * b + 16)
                then(dve.tensor_reduce(amax[:, :], blocks(W[k][:, :]), AX.X, ALU.max, apply_absolute_value=True))
                yield
                then(dve.tensor_scalar(scale[:, k, :], amax[:, :], 1.0 / FP8_MAX, TINY, ALU.mult, ALU.max))
                dve.tensor_reduce(smax[:, k:k + 1], scale[:, k, :], AX.X, ALU.max).then_inc(smax_ready, 1)
                then(dve.reciprocal(rscale[:, :], scale[:, k, :]))
                dve.tensor_tensor(blocks(W[k][:, :]), blocks(W[k][:, :]), each_block(rscale[:, :]),
                                  ALU.mult).then_inc(wv_ready, 1)
                yield

            def unit_round(b, k):
                u = unit(b, k)
                dve.wait_ge(umax_ready, 3 * b + (k + 1))
                power_of_two(pow2[:, :], rpow2[:, :], umax[:, k:k + 1])
                dve.tensor_scalar(unscale[:, k, bass.ds(b, 1)], pow2[:, :], 1.0 / ROOM,
                                  1.0 / X_SCALE if k < 2 else 1.0, ALU.mult, ALU.mult)
                dve.tensor_scalar(dscale[:, :], scale[:, k, :], rpow2[:, 0:1], -ROOM, ALU.mult, ALU.mult)
                dve.wait_ge(wv_ready, u + 1)
                dve.wait_ge(wabs_ready, u + 1)
                round_e4m3(W[k][:, :], absW[:, :], (wabs_used, u + 1))
                yield
                dve.tensor_tensor(blocks(W[k][:, :]), blocks(W[k][:, :]), each_block(dscale[:, :]),
                                  ALU.mult).then_inc(wd_ready, 1)
                yield

            def all_of(steps):
                for _ in steps:
                    pass

            def hidden_of(n, pair, dst, factor):
                dve.wait_ge(silu_ready, n + 1)
                dve.wait_ge(up_ready, n + 1)
                dve.scalar_tensor_tensor(dst, G[2 * pair + 1][:, :], factor, silu[:, pair, :],
                                         ALU.mult, ALU.mult).then_inc(h_ready, 1)

            def turn(b, attention=True, products=True):
                def hidden_tile(r):
                    if products:
                        hidden_of(LT * b + (r - LT), r % 2, h[:, r, bass.ds((b - 1) * 512, 512)], now_unscale[:, 1:2])

                def add_attention(lt):
                    dve.wait_ge(xm_ready, LT * b + (lt + 1))
                    dve.tensor_tensor(X[:, lt, :], X[:, lt, :], AB[lt % 2][:, :], ALU.add).then_inc(xm_taken, 1)

                def row_max(nt):
                    dve.wait_ge(energy_ready, LT * b + (nt + 1))
                    dve.tensor_reduce(nmax[:, nt:nt + 1], AB[nt % 2][:, :], AX.X, ALU.max, negate=True).then_inc(nmax_ready, 1)

                def divide_rows():
                    dve.wait_ge(att_taken, 14 * b + 6)
                    then(dve.reciprocal(rsum[:, :], esum[:, :]))
                    for nt in range(LT):
                        dve.tensor_scalar(probs[:, nt, :], probs[:, nt, :], rsum[:, nt:nt + 1], None,
                                          ALU.mult).then_inc(probs_ready, 1)

                if products:
                    dve.wait_ge(h_ready, LT * b + (2 - LT))
                    dve.tensor_copy(now_unscale[:, :], unscale[:, 0:2, bass.ds(b - 1, 1)]).then_inc(unscale_ready, 1)
                    dve.wait_ge(unscale_ready, b)
                if not attention:
                    stats_of_row(FIRST)
                    hidden_tile(0)
                    scale_row(FIRST)
                    round_row(FIRST)
                    hidden_tile(1)
                    hidden_tile(2)
                    for _ in scale_hidden(0):
                        pass
                    hidden_tile(3)
                    return
                all_of(unit_scale(b, 0))
                gate = unit_round(b, 0)
                if products:
                    row_max(0)
                    row_max(1)
                    next(gate)
                    hidden_tile(0)
                dve.wait_ge(x_in, 16 * b + 16)
                row_stats(b)
                if products:
                    row_max(2)
                    row_max(3)
                    next(gate)
                    up = unit_scale(b, 1)
                    next(up)
                    divide_rows()
                    next(up)
                    up = unit_round(b, 1)
                    down = unit_scale(b, 2)
                    next(down)
                    next(up)
                    add_attention(0)
                    hidden_tile(1)
                    hidden_tile(2)
                    add_attention(1)
                    next(up)
                    next(down)
                    down = unit_round(b, 2)
                    next(down)
                    add_attention(2)
                    add_attention(3)
                    next(down)
                    hidden_tile(3)
                else:
                    for nt in range(LT):
                        row_max(nt)
                    divide_rows()
                    all_of(gate)
                    add_attention(0)
                    up = unit_scale(b, 1)
                    next(up)
                    add_attention(1)
                    next(up)
                    up = unit_round(b, 1)
                    next(up)
                    add_attention(2)
                    add_attention(3)
                    dve.wait_ge(xm_taken, LT)
                    row_stats(0)
                    next(up)

            dve.wait_ge(consts_in, 80)
            dve.tensor_scalar(neg_id[:, :], idf[:, :], -1.0, None, ALU.mult).then_inc(const_ready, 1)
            dve.sem_inc(h_ready, 2)
            turn(0, products=False)
            for half, ready in enumerate((rows0_v, wv_ready)):
                dve.wait_ge(rows0_ready, 2 * half + 2)
                rows, cols = rows0_half(half)
                block_scales(rows, amax[:, cols], xscale[:, cols])
                dve.tensor_scalar(dscale[:, cols], xscale[:, cols], -X_SCALE, None, ALU.mult)
                then(dve.reciprocal(rscale[:, cols], xscale[:, cols]))
                dve.tensor_tensor(blocks(rows), blocks(rows), each_block(rscale[:, cols]), ALU.mult).then_inc(ready, 1)
            for half, (abs_ready, count, done) in enumerate(((rows0_abs, 1, rows0_d), (wabs_ready, ROWS0 + 1, wd_ready))):
                rows, cols = rows0_half(half)
                dve.wait_ge(abs_ready, count)
                round_e4m3(rows, absW[:, half * UNIT // 2:(half + 1) * UNIT // 2],
                           (wabs_used, ROWS0 + 1) if half else None)
                dve.tensor_tensor(blocks(rows), blocks(rows), each_block(dscale[:, cols]), ALU.mult).then_inc(done, 1)
            dve.wait_ge(wd_ready, ROWS0 + 1)
            all_of(unit_scale(0, 2))
            all_of(unit_round(0, 2))
            with dve.Fori(1, B) as b:
                own.enter(b - 1, TURN_STEPS)
                turn(b)
                own.leave(B - 1)

            def stats_of_row(r):
                dve.wait_ge(row_loaded, 16 * (r - (FIRST - 1)))
                then(dve.bn_stats(xstats[:, :], row_in))
                if not isinstance(r, int):
                    carry_wait()
                dve.bn_aggr(xmv[:, :], xstats[:, :]).then_inc(xs_ready, 1)

            def scale_row(r):
                dve.wait_ge(xnorm_ready, r - (FIRST - 1))
                block_scales(xw, xamax[:, :], xscale[:, 0:XB])
                dve.tensor_scalar(xdscale[:, :], xscale[:, 0:XB], -X_SCALE, None, ALU.mult)
                then(dve.reciprocal(xrscale[:, :], xscale[:, 0:XB]))
                dve.tensor_tensor(blocks(xw), blocks(xw), each_block(xrscale[:, :]), ALU.mult).then_inc(xv_ready, 1)

            def round_row(r):
                dve.wait_ge(xabs_ready, r - (FIRST - 1))
                round_e4m3(xw, absX)
                dve.tensor_tensor(blocks(xw), blocks(xw), each_block(xdscale[:, :]), ALU.mult).then_inc(xd_ready, 1)

            def scale_hidden(j, turned_before=None):
                rows = h[:, j % RING, :]
                hw = hidden_rows(j)
                then(dve.tensor_reduce(amax[:, :], blocks(rows), AX.X, ALU.max, apply_absolute_value=True))
                yield
                then(dve.tensor_scalar(scale[:, 0, :], amax[:, :], 1.0 / FP8_MAX, TINY, ALU.mult, ALU.max))
                then(dve.tensor_reduce(smax[:, 0:1], scale[:, 0, :], AX.X, ALU.max))
                power_of_two(hpow2[:, :], hrpow2[:, :], smax[:, 0:1])
                dve.tensor_scalar(dscale[:, :], scale[:, 0, :], hrpow2[:, 0:1], -ROOM, ALU.mult, ALU.mult)
                then(dve.reciprocal(rscale[:, :], scale[:, 0, :]))
                if turned_before is not None:
                    dve.wait_ge(turned, 4 * turned_before + 4 * (UNITS + 1))
                dve.tensor_tensor(blocks(hw), blocks(rows), each_block(rscale[:, :]), ALU.mult).then_inc(hv_ready, 1)
                yield

            def round_hidden(j):
                hw = hidden_rows(j)
                dve.wait_ge(habs_ready, j + 1)
                round_e4m3(hw, absW[:, :])
                then(dve.tensor_scalar(odown_of(j), unscale[:, 2, :], hpow2[:, 0:1], 1.0 / ROOM, ALU.mult, ALU.mult))
                dve.tensor_tensor(blocks(hw), blocks(hw), each_block(dscale[:, :]), ALU.mult).then_inc(hd_ready, 1)

            def result_of(j):
                dve.wait_ge(residual_loaded, 16 * j + 16)
                dve.wait_ge(down_ready, j + 1)
                for n in range(HT):
                    cols = slice(n * P, (n + 1) * P)
                    last = dve.scalar_tensor_tensor(row_out[:, cols], down_bank(j)[:, cols], odown_of(j)[:, n:n + 1],
                                                    row_out[:, cols], ALU.mult, ALU.add)
                last.then_inc(down_taken, 1)

            turn(B, attention=False)

            def slot(r, result=True, last=False):
                def chunk(c):
                    hidden_of(4 * r + c, c % 2, h[:, r % RING, c * 512:(c + 1) * 512], unscale[:, 1, c:c + 1])

                if result:
                    result_of(r - (RING + 1))
                    dve.wait_ge(down_taken, r - RING)
                round_hidden(r - RING)
                if not last:
                    stats_of_row(r + 1)
                chunk(0)
                chunk(1)
                if last:
                    all_of(scale_hidden(TAIL))
                    round_hidden(TAIL)
                    chunk(2)
                    all_of(scale_hidden(TAIL + 1))
                    chunk(3)
                else:
                    scale_row(r + 1)
                    chunk(2)
                    round_row(r + 1)
                    chunk(3)
                    all_of(scale_hidden(r - (RING - 1), turned_before=r - RING))

            @contextmanager
            def fori(first, end):
                with dve.Fori(first, end) as r:
                    own.enter(r - first, SLOT_STEPS)
                    yield r
                    own.leave(end - first)

            run_slots(slot, fori)
            scale_14 = scale_hidden(TAIL + 2, turned_before=TAIL - 1)
            next(scale_14)
            round_hidden(TAIL + 1)
            result_of(TAIL - 1)
            next(scale_14)
            scale_15 = scale_hidden(TAIL + 3, turned_before=TAIL)
            next(scale_15)
            result_of(TAIL)
            round_hidden(TAIL + 2)
            next(scale_15)
            result_of(TAIL + 1)
            round_hidden(TAIL + 3)
            result_of(TAIL + 2)
            result_of(TAIL + 3)


def kernel(x, ctx_1024, L0_xattn_Wq, L0_xattn_bq, L0_xattn_Wk, L0_xattn_bk, L0_ffn_gate_w, L0_ffn_up_w, L0_ffn_down_w):
    import numpy as np
    import concourse.bacc as bacc
    from concourse.bass_utils import run_bass_kernel_spmd

    arrays = {
        "x": np.ascontiguousarray(x),
        "ctxT": np.ascontiguousarray(np.transpose(ctx_1024, (0, 2, 1))),
        "wqT": np.ascontiguousarray(np.transpose(L0_xattn_Wq)),
        "bq": np.ascontiguousarray(np.reshape(L0_xattn_bq, (-1, 1))),
        "wkT": np.ascontiguousarray(np.transpose(L0_xattn_Wk)),
        "bk": np.ascontiguousarray(np.reshape(L0_xattn_bk, (-1, 1))),
        "gate_w": np.ascontiguousarray(L0_ffn_gate_w),
        "up_w": np.ascontiguousarray(L0_ffn_up_w),
        "down_w": np.ascontiguousarray(L0_ffn_down_w),
        "ident": np.eye(P, dtype=np.float32),
    }
    nc = bacc.Bacc("TRN2", target_bir_lowering=False, num_devices=1)
    args = [nc.dram_tensor(f"in_{n}", a.shape, mybir.dt.from_np(a.dtype), kind="ExternalInput").ap()
            for n, a in arrays.items()]
    out = nc.dram_tensor("out_y", arrays["x"].shape, F32, kind="ExternalOutput").ap()
    xattn_ffn(nc, *args, out)
    r = run_bass_kernel_spmd(nc, [{f"in_{n}": a for n, a in arrays.items()}], core_ids=[0])
    return r.results[0]["out_y"]
```

```python
from contextlib import ExitStack, contextmanager

import concourse.bass as bass
from concourse import mybir

F32 = mybir.dt.float32
BF16 = mybir.dt.bfloat16
F16 = mybir.dt.float16
I32 = mybir.dt.int32
ALU = mybir.AluOpType
ACT = mybir.ActivationFunctionType
AX = mybir.AxisListType

P = 128
BLOCK = 32
FP8_MAX = 448.0
TINY = 1e-30
LN_EPS = 1e-5
MAGIC = float(2 ** 20)
MAGIC_FLOOR = 1.5 * 2 ** 14
EXPONENT_BITS = 0x7F800000
X_SCALE = float(2 ** 10)
ROOM = 64.0
TURN_STEPS = 20
SLOT_STEPS = 15


def xattn_ffn(nc, x, ctxT, wqT, bq, wkT, bk, gate_w, up_w, down_w, ident, out):
    B, L, H = x.shape
    C = ctxT.shape[1]
    I = gate_w.shape[0]
    LT = L // P
    HT = H // P
    CT = C // P
    IT = I // P
    CH = I // 512
    RT = B * LT
    UNIT = 2048
    GROUPS = UNIT // 512
    RING = LT
    assert L == H == 512 and C % P == 0 and CH == B and HT == B and IT == 4 * GROUPS and RT > 2 * RING

    x_rows = x.rearrange("b (t p) h -> b p t h", p=P)
    out_rows = out.rearrange("b (t p) h -> (b t) p h", p=P)
    ctx_cols = ctxT.rearrange("b (t p) n -> b p t n", p=P)
    gate_rows = gate_w.rearrange("(c t p) h -> c p t h", p=P, t=4)
    up_rows = up_w.rearrange("(c t p) h -> c p t h", p=P, t=4)
    down_rows = down_w.rearrange("(c p) i -> c p i", p=P)
    x1_dram = nc.dram_tensor("x1_dram", (RT, P, H), F32, kind="Internal").ap()

    with ExitStack() as stack:
        def sb(name, shape, dt):
            return stack.enter_context(nc.sbuf_tensor(name, shape, dt))

        def bank(name):
            return stack.enter_context(nc.psum_tensor(name, [P, 512], F32))

        def sem(name):
            return stack.enter_context(nc.semaphore(name))

        gu_hi = sb("gu_hi", [P, HT, 2, CH, 512], F16)
        gu_lo = sb("gu_lo", [P, HT, 2, CH, 512], F16)
        dn_hi = sb("dn_hi", [P, IT, H], F16)
        dn_lo = sb("dn_lo", [P, IT, H], F16)
        X = sb("X", [P, LT, H], F32)
        h = sb("h", [P, RING, UNIT], F32)
        W = [sb(f"W{k}", [P, UNIT], F32) for k in range(3)]
        absW = sb("absW", [P, UNIT], BF16)
        AT = sb("AT", [P, HT, 512], F32)
        R1 = sb("R1", [P, 2, 512], F32)
        R2 = sb("R2", [P, 2, 512], F32)
        xT = sb("xT", [P, 2, RING, 512], F16)
        xr = sb("xr", [P, 2, 512], F16)
        silu = sb("silu", [P, 2, 512], F32)
        wq_sb = sb("wq_sb", [P, CT, P], F32)
        wk_sb = sb("wk_sb", [P, CT, P], F32)
        bq_sb = sb("bq_sb", [P, 1], F32)
        bk_sb = sb("bk_sb", [P, 1], F32)
        idf = sb("idf", [P, P], F32)
        neg_id = sb("neg_id", [P, P], F16)
        NB = UNIT // BLOCK
        amax = sb("amax", [P, NB], F32)
        scale = sb("scale", [P, 3, NB], F32)
        rscale = sb("rscale", [P, NB], F32)
        dscale = sb("dscale", [P, NB], F32)
        smax = sb("smax", [P, 3], F32)
        umax = sb("umax", [P, 3], F32)
        pow2 = sb("pow2", [P, 1], F32)
        rpow2 = sb("rpow2", [P, 1], F32)
        unscale = sb("unscale", [P, 3, 4], F32)
        now_unscale = sb("now_unscale", [P, 2], F32)
        stats = sb("stats", [P, LT, 6], F32)
        mv = sb("mv", [P, LT, 2], F32)
        veps = sb("veps", [P, LT], F32)
        rstd = sb("rstd", [P, LT], F32)
        nmean = sb("nmean", [P, LT], F32)
        nmr = sb("nmr", [P, LT], F32)
        mhalf = sb("mhalf", [P, LT], F32)
        pool_idle = sb("pool_idle", [P, 4], F32)
        dve_idle = sb("dve_idle", [P, 1], F32)
        nmax = sb("nmax", [P, LT], F32)
        esum = sb("esum", [P, LT], F32)
        rsum = sb("rsum", [P, LT], F32)
        xstats = sb("xstats", [P, 6], F32)
        xmv = sb("xmv", [P, 2], F32)
        XB = H // BLOCK
        xamax = sb("xamax", [P, NB], F32)
        xscale = sb("xscale", [P, NB], F32)
        xrscale = sb("xrscale", [P, XB], F32)
        xdscale = sb("xdscale", [P, XB], F32)
        hpow2 = sb("hpow2", [P, 1], F32)
        hrpow2 = sb("hrpow2", [P, 1], F32)
        odown = sb("odown", [P, 1 + RING, HT], F32)
        ctx_sb = R1
        XT = R1
        qT, kT = R2[:, 0, :], R2[:, 1, :]
        xn = R2
        probs = h[:, :, 3 * 512:]
        rows0 = h[:, 0, :]
        hT = AT[:, :, :].bitcast(F16).rearrange("p g (t n) -> p (g t) n", n=P)
        hT = hT.rearrange("p (a t) n -> p a t n", a=2)
        x_parts = W[0][:, H:2 * H].bitcast(F16).rearrange("p (a n) -> p a n", a=2)
        xT_hi, xT_lo = xT[:, 0, :, :], xT[:, 1, :, :]
        xw = R2[:, 0, :]
        absX = R1[:, 0, :].bitcast(BF16)[:, 0:512]
        row_in, row_out = W[0][:, 0:H], X[:, 1, :]

        G = [bank(f"G{i}") for i in range(4)]
        TB = [bank(f"TB{i}") for i in range(2)]
        AB = [bank(f"AB{i}") for i in range(2)]

        consts_in = sem("consts_in")
        x_in = sem("x_in")
        ctx_in = sem("ctx_in")
        w_in = [sem(f"w_in{k}") for k in range(3)]
        x1_written = sem("x1_written")
        row_loaded = sem("row_loaded")
        xr_in = sem("xr_in")
        hT_in = sem("hT_in")
        residual_loaded = sem("residual_loaded")
        out_written = sem("out_written")
        dve_step = sem("dve_step")
        pool_step = sem("pool_step")
        const_ready = sem("const_ready")
        stats_ready = sem("stats_ready")
        rstd_ready = sem("rstd_ready")
        xn_ready = sem("xn_ready")
        att_ready = sem("att_ready")
        att_taken = sem("att_taken")
        energy_ready = sem("energy_ready")
        nmax_ready = sem("nmax_ready")
        probs_ready = sem("probs_ready")
        xm_ready = sem("xm_ready")
        xm_taken = sem("xm_taken")
        rows0_ready = sem("rows0_ready")
        rows0_v = sem("rows0_v")
        rows0_abs = sem("rows0_abs")
        rows0_d = sem("rows0_d")
        smax_ready = sem("smax_ready")
        umax_ready = sem("umax_ready")
        wv_ready = sem("wv_ready")
        wabs_ready = sem("wabs_ready")
        wabs_used = sem("wabs_used")
        wd_ready = sem("wd_ready")
        turned = sem("turned")
        hi_ready = sem("hi_ready")
        rest_ready = sem("rest_ready")
        lo_ready = sem("lo_ready")
        xs_ready = sem("xs_ready")
        xr_ready = sem("xr_ready")
        xnorm_ready = sem("xnorm_ready")
        xv_ready = sem("xv_ready")
        xabs_ready = sem("xabs_ready")
        xd_ready = sem("xd_ready")
        xhi_ready = sem("xhi_ready")
        xlo_ready = sem("xlo_ready")
        gate_ready = sem("gate_ready")
        unscale_ready = sem("unscale_ready")
        up_ready = sem("up_ready")
        silu_ready = sem("silu_ready")
        h_ready = sem("h_ready")
        hv_ready = sem("hv_ready")
        habs_ready = sem("habs_ready")
        hd_ready = sem("hd_ready")
        hhi_ready = sem("hhi_ready")
        hlo_ready = sem("hlo_ready")
        down_ready = sem("down_ready")
        down_taken = sem("down_taken")

        class Steps:

            def __init__(self, s):
                self.s, self.base, self.n, self.turn, self.each = s, 0, 0, 0, 0

            def done(self, instruction):
                instruction.then_inc(self.s, 1)
                self.n += 1

            @property
            def value(self):
                return self.turn * self.each + (self.base + self.n)

            def enter(self, turn, each):
                self.base, self.n, self.turn, self.each = self.base + self.n, 0, turn, each

            def leave(self, turns):
                assert self.n == self.each, (self.n, self.each)
                self.base, self.n, self.turn, self.each = self.base + turns * self.each, 0, 0, 0

        ROWS0 = 2

        def unit(b, k):
            return (0, 1, 3)[k] if isinstance(b, int) and b == 0 else 3 * b + (k + 1)

        UNITS = 3 * B + 1

        def rows0_half(half):
            return (rows0[:, half * UNIT // 2:(half + 1) * UNIT // 2], slice(half * NB // 2, (half + 1) * NB // 2))

        def group(u, g):
            return g % 2, 4 * u + g

        TAIL = RT - RING

        def unit_part(gu, dn, k, g, b):
            if k < 2:
                return gu[:, g, k, b, :]
            return dn[:, 4 * g:4 * g + 4, bass.ds(b * P, P)]

        FIRST, LAST = RING, RT - 1

        def run_slots(slot, fori):
            slot(FIRST, result=False)
            with fori(FIRST + 1, LAST) as r:
                slot(r)
            slot(LAST, last=True)

        def hidden_rows(j):
            return W[(0, 1, 2, 0)[j - TAIL] if isinstance(j, int) and j >= TAIL else 1][:, :]

        hidden_parts = W[2][:, :].bitcast(F16).rearrange("p (a n) -> p a n", a=2)

        def tail_unit(j):
            return UNITS + j - TAIL

        def down_bank(j):
            return AB[(j - TAIL + 1) % 2 if isinstance(j, int) and j >= TAIL else 0]

        def odown_of(j):
            return odown[:, j - TAIL + 1 if isinstance(j, int) and j >= TAIL else 0, :]

        block = stack.enter_context(nc.Block())

        @block.sync
        def _(sp):
            def load_unit(b, k):
                rows = (gate_rows, up_rows, down_rows)[k]
                dst = W[k][:, :] if k == 2 else W[k][:, :].rearrange("p (t n) -> p t n", n=H)
                sp.dma_start(dst, rows[b]).then_inc(w_in[k], 16)

            def store_rows(b):
                sp.wait_ge(xm_taken, LT * b + LT)
                rows = x1_dram[bass.ds(b * LT, LT)].rearrange("t p h -> p t h")
                sp.dma_start(rows, X[:, :, :]).then_inc(x1_written, 16)

            def loads(b):
                sp.wait_ge(turned, group(unit(b - 1, 0), 4)[1])
                load_unit(b, 0)
                sp.wait_ge(xm_ready, LT * b)
                sp.dma_start(ctx_sb[:, :, :], ctx_cols[b]).then_inc(ctx_in, 16)
                store_rows(b - 1)
                sp.wait_ge(x1_written, 16 * b)
                if isinstance(b, int):
                    sp.wait_ge(rows0_ready, LT)
                sp.dma_start(X[:, :, :], x_rows[b]).then_inc(x_in, 16)
                sp.wait_ge(turned, group(unit(b - 1, 1), 4)[1])
                load_unit(b, 1)
                sp.wait_ge(turned, group(unit(b - 1, 2), 4)[1])
                load_unit(b, 2)

            sp.dma_start(ctx_sb[:, :, :], ctx_cols[0]).then_inc(ctx_in, 16)
            load_unit(0, 0)
            for dst, src in ((wq_sb[:, :, :], wqT.rearrange("(t p) d -> p t d", p=P)),
                             (wk_sb[:, :, :], wkT.rearrange("(t p) d -> p t d", p=P)),
                             (bq_sb[:, :], bq), (bk_sb[:, :], bk), (idf[:, :], ident)):
                sp.dma_start(dst, src).then_inc(consts_in, 16)
            sp.dma_start(X[:, :, :], x_rows[0]).then_inc(x_in, 16)
            load_unit(0, 1)
            load_unit(0, 2)
            loads(1)
            with sp.Fori(2, B) as b:
                loads(b)
            sp.wait_ge(turned, group(unit(B - 1, 0), 4)[1])
            sp.dma_start(row_in, x1_dram[FIRST]).then_inc(row_loaded, 16)
            store_rows(B - 1)
            sp.wait_ge(x1_written, 16 * B)

            def turn_row():
                sp.dma_start_transpose(xr[:, :, :].rearrange("p a (t n) -> p (a t) n", n=P),
                                       x_parts.rearrange("p a n -> p (a n)")).then_inc(xr_in, 16)

            def load_row(r):
                sp.dma_start(row_in, x1_dram[r]).then_inc(row_loaded, 16)

            def load_residual(j):
                sp.dma_start(row_out, x1_dram[j]).then_inc(residual_loaded, 16)

            def turn_hidden():
                for part in range(2):
                    sp.dma_start_transpose(hT[:, part, :, :], hidden_parts[:, part, :]).then_inc(hT_in, 16)

            def store_out(j):
                sp.wait_ge(down_taken, j + 1)
                sp.dma_start(out_rows[j], row_out).then_inc(out_written, 16)

            def slot(r):
                if not isinstance(r, int) or r > FIRST:
                    store_out(r - (RING + 1))
                sp.wait_ge(hlo_ready, r - (RING - 1))
                if not isinstance(r, int) or r > FIRST:
                    sp.wait_ge(out_written, 16 * r - 16 * RING)
                load_residual(r - RING)
                turn_hidden()
                if not isinstance(r, int) or r < LAST:
                    sp.wait_ge(xlo_ready, r - (FIRST - 2))
                    sp.wait_ge(up_ready, 4 * r + 4)
                    if not isinstance(r, int) or r < LAST - 1:
                        load_row(r + 2)
                    turn_row()

            sp.wait_ge(xlo_ready, 1)
            load_row(FIRST + 1)
            turn_row()
            slot(FIRST)
            with sp.Fori(FIRST + 1, LAST - 1) as r:
                slot(r)
            slot(LAST - 1)
            slot(LAST)
            for j in range(TAIL - 1, RT):
                store_out(j)
                sp.wait_ge(out_written, 16 * (j + 1))
                if j + 1 < RT:
                    load_residual(j + 1)

        @block.gpsimd
        def _(pool):
            own = Steps(pool_step)

            def carry_wait(n):
                nc.gpsimd.tensor_tensor(pool_idle[:, n:n + 1], mhalf[:, 0:1], mhalf[:, 0:1], ALU.mult)

            def inverse_std(m, n, ready):
                own.done(nc.gpsimd.tensor_scalar(veps[:, 0:n], m[:, :, 1], LN_EPS, 1.0, ALU.add, ALU.mult))
                own.done(nc.gpsimd.tensor_scalar(nmean[:, 0:n], m[:, :, 0], -1.0, 0.0, ALU.mult, ALU.add))
                pool.wait_ge(pool_step, own.value)
                own.done(nc.gpsimd.tensor_tensor(rstd[:, 0:n], veps[:, 0:n], mhalf[:, 0:n], ALU.pow))
                pool.wait_ge(pool_step, own.value)
                nc.gpsimd.tensor_tensor(nmr[:, 0:n], nmean[:, 0:n], rstd[:, 0:n], ALU.mult).then_inc(ready, 1)

            def unit_max(b, k):
                pool.wait_ge(smax_ready, 3 * b + (k + 1))
                carry_wait(1 + k)
                nc.gpsimd.partition_all_reduce(umax[:, k:k + 1], smax[:, k:k + 1], P,
                                               bass.bass_isa.ReduceOp.max).then_inc(umax_ready, 1)

            own.done(nc.gpsimd.memset(mhalf[:, :], -0.5))
            pool.wait_ge(pool_step, own.value)
            unit_max(0, 0)
            pool.wait_ge(stats_ready, 1)
            inverse_std(mv, LT, rstd_ready)
            unit_max(0, 1)
            pool.wait_ge(stats_ready, 2)
            inverse_std(mv, LT, rstd_ready)
            unit_max(0, 2)
            with pool.Fori(1, B) as b:
                own.enter(b - 1, 3)
                unit_max(b, 0)
                pool.wait_ge(stats_ready, b + 2)
                carry_wait(0)
                inverse_std(mv, LT, rstd_ready)
                unit_max(b, 1)
                unit_max(b, 2)
                own.leave(B - 1)
            with pool.Fori(0, RT - FIRST) as n:
                own.enter(n, 3)
                pool.wait_ge(xs_ready, n + 1)
                carry_wait(0)
                inverse_std(xmv[:, :].unsqueeze(1), 1, xr_ready)
                own.leave(RT - FIRST)

        @block.tensor
        def _(pe):
            def turn4(dst, tiles):
                for j, t in enumerate(tiles):
                    last = pe.matmul(dst[:, j * P:(j + 1) * P], t, idf[:, :], is_transpose=True,
                                     start=(j == 0), stop=(j == 3))
                return last

            def turn_group(u, g, tiles):
                which, n = group(u, g)
                if not isinstance(n, int) or n >= 2:
                    pe.wait_ge(lo_ready, n - 1)
                turn4(TB[which], tiles).then_inc(turned, 1)

            def subtract_hi(u, g, hi):
                which, n = group(u, g)
                pe.wait_ge(hi_ready, n + 1)
                pe.matmul(TB[which][:, :], neg_id[:, :], hi, start=False, stop=True,
                          skip_group_check=True).then_inc(rest_ready, 1)

            def half_products(pair, g, xhi, xlo, chunk):
                dst = G[2 * pair + g]
                m = 0
                for j in range(HT):
                    for a, w in ((xhi, gu_hi), (xhi, gu_lo), (xlo, gu_hi)):
                        last = pe.matmul(dst[:, :], a[:, j * P:(j + 1) * P], w[:, j, g, chunk, :],
                                         start=(m == 0), stop=(m == 3 * HT - 1))
                        m += 1
                last.then_inc((gate_ready, up_ready)[g], 1)

            def turn_unit(b, k):
                u = unit(b, k)
                pe.wait_ge(wd_ready, 3 * b + (k + 1))
                for pair in range(GROUPS // 2):
                    for g in (2 * pair, 2 * pair + 1):
                        if k < 2:
                            tiles = [W[k][:, t * H + g * P:t * H + (g + 1) * P] for t in range(4)]
                        else:
                            tiles = [W[k][:, (4 * g + t) * P:(4 * g + t + 1) * P] for t in range(4)]
                        turn_group(u, g, tiles)
                    yield
                    for g in (2 * pair, 2 * pair + 1):
                        subtract_hi(u, g, unit_part(gu_hi, dn_hi, k, g, b))
                    yield

            def turn(b, attention=True, products=True):
                taken = 14 * b
                nothing = iter(())

                def half(r, g):
                    if products:
                        if r == 0 and g == 0:
                            pe.wait_ge(lo_ready, group(3 * b - 1, 4)[1])
                        if g == 0:
                            pe.wait_ge(h_ready, LT * b + (r - LT + 1))
                        half_products(r % 2, g, xT_hi[:, r, :], xT_lo[:, r, :], b - 1)

                def attend(step, *args):
                    if attention:
                        step(*args)

                def project(i):
                    w = (wq_sb, wk_sb)[i]
                    pe.wait_ge(ctx_in, 16 * b + 16)
                    if not isinstance(b, int):
                        pe.wait_ge(xm_taken, LT * b + (i - 1))
                    for t in range(CT):
                        last = pe.matmul(AB[i][:, :], w[:, t, :], ctx_sb[:, t, :], start=(t == 0), stop=(t == CT - 1))
                    last.then_inc(att_ready, 1)

                def energies(nt):
                    pe.wait_ge(att_taken, taken + max(nt + 1, 2))
                    pe.matmul(AB[nt % 2][:, :], qT[:, nt * P:(nt + 1) * P], kT,
                              start=True, stop=True).then_inc(energy_ready, 1)

                def turn_probs(nt):
                    pe.wait_ge(att_taken, taken + (nt + 7))
                    pe.wait_ge(probs_ready, LT * b + (nt + 1))
                    turn4(AB[nt % 2], [probs[:, nt, j * P:(j + 1) * P] for j in range(HT)]).then_inc(att_ready, 1)

                def turn_rows(lt):
                    if lt < 2:
                        pe.wait_ge(att_taken, taken + (lt + 5))
                    else:
                        pe.wait_ge(xm_taken, LT * b + (lt - 1))
                    pe.wait_ge(xn_ready, LT * b + (lt + 1))
                    turn4(AB[lt % 2], [xn[:, lt % 2, j * P:(j + 1) * P] for j in range(HT)]).then_inc(att_ready, 1)

                def attend_rows(lt, tiles=range(HT)):
                    if tiles[0] == 0:
                        pe.wait_ge(att_taken, taken + max(lt + 11, 12))
                    for j in tiles:
                        last = pe.matmul(AB[lt % 2][:, :], XT[:, lt % 2, j * P:(j + 1) * P], AT[:, j, :],
                                         start=(j == 0), stop=(j == HT - 1))
                    if tiles[-1] == HT - 1:
                        last.then_inc(xm_ready, 1)

                down = turn_unit(b - 1, 2) if products else nothing
                gate, up = (turn_unit(b, 0), turn_unit(b, 1)) if attention else (nothing, nothing)
                half(0, 0)
                attend(project, 0)
                attend(project, 1)
                half(0, 1)
                attend(energies, 0)
                attend(energies, 1)
                half(1, 0)
                next(down, None)
                half(1, 1)
                next(down, None)
                attend(energies, 2)
                attend(energies, 3)
                half(2, 0)
                next(down, None)
                attend(turn_rows, 0)
                attend(turn_rows, 1)
                next(down, None)
                half(2, 1)
                attend(turn_probs, 0)
                attend(turn_probs, 1)
                if products:
                    next(gate, None)
                attend(turn_probs, 2)
                attend(turn_probs, 3)
                if products:
                    next(gate, None)
                attend(attend_rows, 0)
                next(gate, None)
                attend(attend_rows, 1)
                next(gate, None)
                attend(turn_rows, 2)
                attend(turn_rows, 3)
                if not products:
                    next(gate)
                half(3, 0)
                if products:
                    next(up, None)
                attend(attend_rows, 2)
                if products:
                    next(up, None)
                attend(attend_rows, 3, range(HT // 2))
                if products:
                    next(up, None)
                attend(attend_rows, 3, range(HT // 2, HT))
                if products:
                    next(up, None)
                half(3, 1)
                for part in (gate, up):
                    for _ in part:
                        pass

            pe.wait_ge(consts_in, 80)
            pe.wait_ge(const_ready, 1)
            turn(0, products=False)
            for pair in range(2):
                pe.wait_ge(rows0_d, pair + 1)
                for t in (2 * pair, 2 * pair + 1):
                    turn_group(ROWS0, t, [rows0[:, t * H + j * P:t * H + (j + 1) * P] for j in range(HT)])
                for t in (2 * pair, 2 * pair + 1):
                    subtract_hi(ROWS0, t, xT_hi[:, t, :])
            with pe.Fori(1, B) as b:
                turn(b)

            turn(B, attention=False)

            def down_pass(j, g, passes):
                for k in range(4 * g, 4 * g + 4):
                    for a, w in passes:
                        last = pe.matmul(down_bank(j)[:, :], hT[:, a, k, :], (dn_hi, dn_lo)[w][:, k, :],
                                         start=(k == 0 and a == 0 and w == 0), stop=(k == IT - 1 and a == 1))
                if g == 3 and (1, 0) in passes:
                    last.then_inc(down_ready, 1)

            def slot(r, result=True, last=False):
                j = r - RING

                def products(c):
                    pe.wait_ge(h_ready, 4 * r + (c + 1))
                    half_products(c % 2, 0, xr[:, 0, :], xr[:, 1, :], c)
                    half_products(c % 2, 1, xr[:, 0, :], xr[:, 1, :], c)

                pe.wait_ge(xr_in, 16 * r - 16 * (FIRST - 1))
                for c in range(4):
                    products(c)
                pe.wait_ge(hT_in, 32 * j + 32)
                if result:
                    pe.wait_ge(down_taken, j)
                for g in range(GROUPS):
                    down_pass(j, g, ((0, 0), (0, 1), (1, 0)))

            run_slots(slot, pe.Fori)
            groups = [(j, g) for j in range(TAIL, RT) for g in range(GROUPS)]

            def hi_of(g):
                return hT[:, 0, 4 * g:4 * g + 4, :]

            def turn_next(j, g):
                if g == 0:
                    pe.wait_ge(hd_ready, j + 1)
                hw = hidden_rows(j)
                turn_group(tail_unit(j), g, [hw[:, (4 * g + t) * P:(4 * g + t + 1) * P] for t in range(4)])

            for n, (j, g) in enumerate(groups):
                if n == 0:
                    turn_next(j, g)
                    subtract_hi(tail_unit(j), g, hi_of(g))
                if g == 0 and j > TAIL:
                    pe.wait_ge(down_taken, j - 1)
                down_pass(j, g, ((0, 0), (0, 1)))
                if n + 1 < len(groups):
                    turn_next(*groups[n + 1])
                pe.wait_ge(lo_ready, group(tail_unit(j), g)[1] + 1)
                down_pass(j, g, ((1, 0),))
                if n + 1 < len(groups):
                    following = groups[n + 1]
                    subtract_hi(tail_unit(following[0]), following[1], hi_of(following[1]))

        @block.scalar
        def _(act):
            def take(dst, src, ready, count, signal, func=ACT.Copy, **kw):
                act.wait_ge(ready, count)
                nc.scalar.activation(dst, src, func, **kw).then_inc(signal, 1)

            def split_unit(u, dst, as_tiles=False, at_once=2):
                for first in range(0, GROUPS, at_once):
                    for part, ready, signal in ((0, turned, hi_ready), (1, rest_ready, lo_ready)):
                        for g in range(first, first + at_once):
                            which, n = group(u, g)
                            src = TB[which][:, :]
                            if as_tiles:
                                src = src.rearrange("p (j n) -> p j n", n=P)
                            take(dst(part, g), src, ready, n + 1, signal)
                        yield

            def split_weight(b, k):
                def dst(part, g):
                    return unit_part((gu_hi, gu_lo)[part], (dn_hi, dn_lo)[part], k, g, b)
                return split_unit(unit(b, k), dst, as_tiles=(k == 2))

            def unit_abs(b, k):
                if not isinstance(b, int) or b > 0 or k > 0:
                    act.wait_ge(wabs_used, 3 * b + k)
                act.wait_ge(wv_ready, 3 * b + (k + 1))
                nc.scalar.activation(absW[:, :], W[k][:, :], ACT.Abs, scale=MAGIC).then_inc(wabs_ready, 1)

            def silu_of(n, pair, factor):
                act.wait_ge(gate_ready, n + 1)
                nc.scalar.activation(silu[:, pair, :], G[2 * pair][:, :], ACT.Silu,
                                     scale=factor).then_inc(silu_ready, 1)

            def turn(b, attention=True, products=True):
                def silu_tile(r):
                    if products:
                        if r == 0:
                            act.wait_ge(unscale_ready, b)
                        silu_of(LT * b + (r - LT), r % 2, now_unscale[:, 0:1])

                def take_projection(i):
                    take((qT, kT)[i], AB[i][:, :], att_ready, 10 * b + (i + 1), att_taken,
                         func=ACT.Identity, bias=(bq_sb, bk_sb)[i][:, 0:1])

                def exponentials(nt):
                    act.wait_ge(nmax_ready, LT * b + (nt + 1))
                    nc.scalar.activation(probs[:, nt, :], AB[nt % 2][:, :], ACT.Exp, bias=nmax[:, nt:nt + 1],
                                         accum_out=esum[:, nt:nt + 1]).then_inc(att_taken, 1)

                def take_probs(nt):
                    take(AT[:, :, nt * P:(nt + 1) * P], AB[nt % 2][:, :].rearrange("p (j n) -> p j n", n=P),
                         att_ready, 10 * b + (nt + 5), att_taken)

                def normalize(lt):
                    if lt == 0:
                        act.wait_ge(rstd_ready, b + 1 if isinstance(b, int) and b == 0 else b + 2)
                    nc.scalar.activation(xn[:, lt % 2, :], X[:, lt, :], ACT.Identity,
                                         scale=rstd[:, lt:lt + 1], bias=nmr[:, lt:lt + 1]).then_inc(xn_ready, 1)

                def take_rows(lt):
                    take(XT[:, lt % 2, :], AB[lt % 2][:, :], att_ready, 10 * b + (lt + (3 if lt < 2 else 7)), att_taken)

                down = split_weight(b - 1, 2) if products else iter(())
                gate, up = split_weight(b, 0), split_weight(b, 1)
                if not attention:
                    silu_tile(0)
                    normalize_row(FIRST)
                    next(down)
                    row_abs(FIRST)
                    next(down)
                    row_hi(FIRST)
                    silu_tile(1)
                    next(down)
                    next(down)
                    silu_tile(2)
                    hidden_abs(0)
                    silu_tile(3)
                    return
                silu_tile(0)
                take_projection(0)
                take_projection(1)
                unit_abs(b, 0)
                next(down, None)
                exponentials(0)
                exponentials(1)
                next(down, None)
                exponentials(2)
                exponentials(3)
                normalize(0)
                normalize(1)
                next(down, None)
                take_rows(0)
                take_rows(1)
                next(down, None)
                take_probs(0)
                take_probs(1)
                if products:
                    next(gate, None)
                take_probs(2)
                take_probs(3)
                if products:
                    unit_abs(b, 1)
                    next(gate, None)
                    next(gate, None)
                    silu_tile(1)
                    silu_tile(2)
                normalize(2)
                normalize(3)
                if products:
                    next(gate, None)
                else:
                    next(gate)
                    next(gate)
                take_rows(2)
                take_rows(3)
                if products:
                    next(up, None)
                    unit_abs(b, 2)
                    next(up, None)
                    next(up, None)
                else:
                    next(gate)
                    unit_abs(b, 1)
                    next(gate)
                    normalize_rows0()
                    next(up)
                    next(up)
                    rows0_absolutes(0)
                silu_tile(3)
                for _ in up:
                    pass

            def normalize_rows0():
                act.wait_ge(rstd_ready, 2)
                for lt in range(LT):
                    nc.scalar.activation(rows0[:, lt * H:(lt + 1) * H], X[:, lt, :], ACT.Identity,
                                         scale=rstd[:, lt:lt + 1], bias=nmr[:, lt:lt + 1]).then_inc(rows0_ready, 1)

            def rows0_absolutes(half):
                act.wait_ge(wabs_used, 2)
                act.wait_ge(rows0_v, half + 1)
                nc.scalar.activation(absW[:, half * UNIT // 2:(half + 1) * UNIT // 2], rows0_half(half)[0],
                                     ACT.Abs, scale=MAGIC).then_inc(rows0_abs, 1)

            act.wait_ge(consts_in, 80)
            act.wait_ge(x_in, 16)
            turn(0, products=False)
            rows0_absolutes(1)
            for _ in split_unit(ROWS0, lambda part, t: (xT_hi, xT_lo)[part][:, t, :]):
                pass
            act.wait_ge(rows0_d, 2)
            unit_abs(0, 2)
            with act.Fori(1, B) as b:
                turn(b)

            def normalize_row(r):
                act.wait_ge(xr_ready, r - (FIRST - 1))
                nc.scalar.activation(xw, row_in, ACT.Identity,
                                     scale=rstd[:, 0:1], bias=nmr[:, 0:1]).then_inc(xnorm_ready, 1)

            def row_abs(r):
                act.wait_ge(xv_ready, r - (FIRST - 1))
                nc.scalar.activation(absX, xw, ACT.Abs, scale=MAGIC).then_inc(xabs_ready, 1)

            def row_hi(r):
                act.wait_ge(xd_ready, r - (FIRST - 1))
                nc.scalar.activation(x_parts[:, 0, :], xw, ACT.Copy).then_inc(xhi_ready, 1)

            def hidden_abs(j):
                act.wait_ge(hv_ready, j + 1)
                nc.scalar.activation(absW[:, :], hidden_rows(j), ACT.Abs, scale=MAGIC).then_inc(habs_ready, 1)

            turn(B, attention=False)

            def hidden_hi(j):
                act.wait_ge(hd_ready, j + 1)
                if not isinstance(j, int) or j > 0:
                    act.wait_ge(hT_in, 32 * j)
                nc.scalar.activation(hidden_parts[:, 0, :], hidden_rows(j), ACT.Copy).then_inc(hhi_ready, 1)

            def slot(r, result=True, last=False):
                j = r - RING
                if result:
                    hidden_abs(j)
                silu_of(4 * r, 0, unscale[:, 0, 0:1])
                hidden_hi(j)
                silu_of(4 * r + 1, 1, unscale[:, 0, 1:2])
                if last:
                    hidden_abs(TAIL)
                else:
                    normalize_row(r + 1)
                silu_of(4 * r + 2, 0, unscale[:, 0, 2:3])
                if not last:
                    row_abs(r + 1)
                    row_hi(r + 1)
                silu_of(4 * r + 3, 1, unscale[:, 0, 3:4])

            run_slots(slot, act.Fori)
            for j in range(TAIL, RT):
                def dst(part, g):
                    return hT[:, part, 4 * g:4 * g + 4, :]
                split = split_unit(tail_unit(j), dst, as_tiles=True, at_once=1)
                for step, _ in enumerate(split):
                    if step == (0, 0, 1, -1)[j - TAIL]:
                        hidden_abs(j + 1)

        @block.vector
        def _(dve):
            own = Steps(dve_step)

            def carry_wait():
                dve.tensor_copy(dve_idle[:, :], bq_sb[:, :])

            def then(instruction):
                own.done(instruction)
                dve.wait_ge(dve_step, own.value)

            def blocks(t):
                return t.rearrange("p (b k) -> p b k", k=BLOCK)

            def each_block(s):
                return s.unsqueeze(2).broadcast_to([P, s.shape[1], BLOCK])

            def block_scales(src, am, sc):
                then(dve.tensor_reduce(am, blocks(src), AX.X, ALU.max, apply_absolute_value=True))
                then(dve.tensor_scalar(sc, am, 1.0 / FP8_MAX, TINY, ALU.mult, ALU.max))

            def power_of_two(p2, rp2, largest):
                then(dve.tensor_scalar(p2.bitcast(I32), largest.bitcast(I32), EXPONENT_BITS, None, ALU.bitwise_and))
                then(dve.reciprocal(rp2, p2))

            def round_e4m3(v, av, read=None):
                then(dve.scalar_tensor_tensor(v, av, MAGIC_FLOOR, v, ALU.max, ALU.add))
                last = dve.scalar_tensor_tensor(v, av, MAGIC_FLOOR, v, ALU.max, ALU.subtract)
                if read is None:
                    then(last)
                else:
                    last.then_inc(read[0], 1)
                    dve.wait_ge(*read)

            def row_stats(n):
                for lt in range(LT):
                    last = dve.bn_stats(stats[:, lt, :], X[:, lt, :])
                then(last)
                if not isinstance(n, int):
                    carry_wait()
                for lt in range(LT):
                    last = dve.bn_aggr(mv[:, lt, :], stats[:, lt, :])
                last.then_inc(stats_ready, 1)

            def unit_scale(b, k):
                dve.wait_ge(w_in[k], 16 * b + 16)
                then(dve.tensor_reduce(amax[:, :], blocks(W[k][:, :]), AX.X, ALU.max, apply_absolute_value=True))
                yield
                then(dve.tensor_scalar(scale[:, k, :], amax[:, :], 1.0 / FP8_MAX, TINY, ALU.mult, ALU.max))
                dve.tensor_reduce(smax[:, k:k + 1], scale[:, k, :], AX.X, ALU.max).then_inc(smax_ready, 1)
                then(dve.reciprocal(rscale[:, :], scale[:, k, :]))
                dve.tensor_tensor(blocks(W[k][:, :]), blocks(W[k][:, :]), each_block(rscale[:, :]),
                                  ALU.mult).then_inc(wv_ready, 1)
                yield

            def unit_round(b, k):
                n = 3 * b + k
                dve.wait_ge(umax_ready, 3 * b + (k + 1))
                power_of_two(pow2[:, :], rpow2[:, :], umax[:, k:k + 1])
                dve.tensor_scalar(unscale[:, k, bass.ds(b, 1)], pow2[:, :], 1.0 / ROOM,
                                  1.0 / X_SCALE if k < 2 else 1.0, ALU.mult, ALU.mult)
                dve.tensor_scalar(dscale[:, :], scale[:, k, :], rpow2[:, 0:1], -ROOM, ALU.mult, ALU.mult)
                dve.wait_ge(wv_ready, n + 1)
                dve.wait_ge(wabs_ready, n + 1)
                round_e4m3(W[k][:, :], absW[:, :], (wabs_used, n + 1))
                yield
                dve.tensor_tensor(blocks(W[k][:, :]), blocks(W[k][:, :]), each_block(dscale[:, :]),
                                  ALU.mult).then_inc(wd_ready, 1)
                yield

            def all_of(steps):
                for _ in steps:
                    pass

            def hidden_of(n, pair, dst, factor):
                dve.wait_ge(silu_ready, n + 1)
                dve.wait_ge(up_ready, n + 1)
                dve.scalar_tensor_tensor(dst, G[2 * pair + 1][:, :], factor, silu[:, pair, :],
                                         ALU.mult, ALU.mult).then_inc(h_ready, 1)

            def keep_unscale(b):
                dve.wait_ge(h_ready, LT * b + 2)
                if not isinstance(b, int):
                    carry_wait()
                dve.tensor_copy(now_unscale[:, :], unscale[:, 0:2, bass.ds(b, 1)]).then_inc(unscale_ready, 1)
                dve.wait_ge(unscale_ready, b + 1)

            def turn(b, attention=True, products=True):
                def hidden_tile(r):
                    if products:
                        hidden_of(LT * b + (r - LT), r % 2, h[:, r, bass.ds((b - 1) * 512, 512)], now_unscale[:, 1:2])

                def add_attention(lt):
                    dve.wait_ge(xm_ready, LT * b + (lt + 1))
                    dve.tensor_tensor(X[:, lt, :], X[:, lt, :], AB[lt % 2][:, :], ALU.add).then_inc(xm_taken, 1)

                def row_max(nt):
                    dve.wait_ge(energy_ready, LT * b + (nt + 1))
                    dve.tensor_reduce(nmax[:, nt:nt + 1], AB[nt % 2][:, :], AX.X, ALU.max,
                                      negate=True).then_inc(nmax_ready, 1)

                def divide_rows():
                    dve.wait_ge(att_taken, 14 * b + 6)
                    then(dve.reciprocal(rsum[:, :], esum[:, :]))
                    for nt in range(LT):
                        dve.tensor_scalar(probs[:, nt, :], probs[:, nt, :], rsum[:, nt:nt + 1], None,
                                          ALU.mult).then_inc(probs_ready, 1)

                if not attention:
                    stats_of_row(FIRST)
                    hidden_tile(0)
                    scale_row(FIRST)
                    round_row(FIRST)
                    row_lo(FIRST)
                    hidden_tile(1)
                    all_of(scale_hidden(0))
                    hidden_tile(2)
                    round_hidden(0)
                    hidden_tile(3)
                    return
                all_of(unit_scale(b, 0))
                gate = unit_round(b, 0)
                if products and isinstance(b, int):
                    row_max(0)
                    row_max(1)
                    next(gate)
                    hidden_tile(0)
                dve.wait_ge(x_in, 16 * b + 16)
                row_stats(b)
                if products and not isinstance(b, int):
                    row_max(0)
                    row_max(1)
                    next(gate)
                    hidden_tile(0)
                if products:
                    row_max(2)
                    row_max(3)
                    next(gate)
                    up = unit_scale(b, 1)
                    next(up)
                    divide_rows()
                    next(up)
                    up = unit_round(b, 1)
                    down = unit_scale(b, 2)
                    next(down)
                    next(up)
                    add_attention(0)
                    hidden_tile(1)
                    add_attention(1)
                    hidden_tile(2)
                    next(up)
                    next(down)
                    down = unit_round(b, 2)
                    next(down)
                    add_attention(2)
                    add_attention(3)
                    next(down)
                    hidden_tile(3)
                    keep_unscale(b)
                else:
                    down = unit_scale(b, 2)
                    for nt in range(LT):
                        row_max(nt)
                    divide_rows()
                    all_of(gate)
                    all_of(unit_scale(b, 1))
                    add_attention(0)
                    add_attention(1)
                    next(down)
                    up = unit_round(b, 1)
                    next(up)
                    add_attention(2)
                    add_attention(3)
                    dve.wait_ge(xm_taken, LT)
                    row_stats(0)
                    next(up)
                    return down

            dve.wait_ge(consts_in, 80)
            dve.tensor_scalar(neg_id[:, :], idf[:, :], -1.0, None, ALU.mult).then_inc(const_ready, 1)
            dve.sem_inc(h_ready, 2)
            down = turn(0, products=False)
            for half in range(2):
                dve.wait_ge(rows0_ready, 2 * half + 2)
                rows, cols = rows0_half(half)
                block_scales(rows, xamax[:, cols], xscale[:, cols])
                dve.tensor_scalar(dscale[:, cols], xscale[:, cols], -X_SCALE, None, ALU.mult)
                then(dve.reciprocal(rscale[:, cols], xscale[:, cols]))
                dve.tensor_tensor(blocks(rows), blocks(rows), each_block(rscale[:, cols]),
                                  ALU.mult).then_inc(rows0_v, 1)
            for half in range(2):
                rows, cols = rows0_half(half)
                dve.wait_ge(rows0_abs, half + 1)
                round_e4m3(rows, absW[:, half * UNIT // 2:(half + 1) * UNIT // 2])
                dve.tensor_tensor(blocks(rows), blocks(rows), each_block(dscale[:, cols]),
                                  ALU.mult).then_inc(rows0_d, 1)
            dve.wait_ge(rows0_d, 2)
            keep_unscale(0)
            next(down)
            all_of(unit_round(0, 2))
            turn(1)
            with dve.Fori(2, B) as b:
                own.enter(b - 2, TURN_STEPS)
                turn(b)
                own.leave(B - 2)

            def stats_of_row(r):
                dve.wait_ge(row_loaded, 16 * (r - (FIRST - 1)))
                then(dve.bn_stats(xstats[:, :], row_in))
                if not isinstance(r, int):
                    carry_wait()
                dve.bn_aggr(xmv[:, :], xstats[:, :]).then_inc(xs_ready, 1)

            def scale_row(r):
                dve.wait_ge(xnorm_ready, r - (FIRST - 1))
                block_scales(xw, xamax[:, 0:XB], xscale[:, 0:XB])
                dve.tensor_scalar(xdscale[:, :], xscale[:, 0:XB], -X_SCALE, None, ALU.mult)
                then(dve.reciprocal(xrscale[:, :], xscale[:, 0:XB]))
                dve.tensor_tensor(blocks(xw), blocks(xw), each_block(xrscale[:, :]), ALU.mult).then_inc(xv_ready, 1)

            def round_row(r):
                dve.wait_ge(xabs_ready, r - (FIRST - 1))
                round_e4m3(xw, absX)
                dve.tensor_tensor(blocks(xw), blocks(xw), each_block(xdscale[:, :]), ALU.mult).then_inc(xd_ready, 1)

            def row_lo(r):
                dve.wait_ge(xhi_ready, r - (FIRST - 1))
                dve.tensor_tensor(x_parts[:, 1, :], xw, x_parts[:, 0, :], ALU.subtract).then_inc(xlo_ready, 1)

            def hidden_lo(j):
                dve.wait_ge(hhi_ready, j + 1)
                dve.tensor_tensor(hidden_parts[:, 1, :], hidden_rows(j), hidden_parts[:, 0, :],
                                  ALU.subtract).then_inc(hlo_ready, 1)

            def scale_hidden(j):
                rows = h[:, j % RING, :]
                hw = hidden_rows(j)
                then(dve.tensor_reduce(amax[:, :], blocks(rows), AX.X, ALU.max, apply_absolute_value=True))
                yield
                then(dve.tensor_scalar(scale[:, 0, :], amax[:, :], 1.0 / FP8_MAX, TINY, ALU.mult, ALU.max))
                then(dve.tensor_reduce(smax[:, 0:1], scale[:, 0, :], AX.X, ALU.max))
                power_of_two(hpow2[:, :], hrpow2[:, :], smax[:, 0:1])
                dve.tensor_scalar(dscale[:, :], scale[:, 0, :], hrpow2[:, 0:1], -ROOM, ALU.mult, ALU.mult)
                then(dve.reciprocal(rscale[:, :], scale[:, 0, :]))
                if isinstance(j, int) and j == TAIL + 2:
                    dve.wait_ge(hT_in, 32 * TAIL)
                elif isinstance(j, int) and j == TAIL + 3:
                    dve.wait_ge(turned, group(tail_unit(TAIL), 4)[1])
                elif not isinstance(j, int):
                    dve.wait_ge(hlo_ready, j)
                dve.tensor_tensor(blocks(hw), blocks(rows), each_block(rscale[:, :]), ALU.mult).then_inc(hv_ready, 1)
                yield

            def round_hidden(j):
                hw = hidden_rows(j)
                dve.wait_ge(habs_ready, j + 1)
                round_e4m3(hw, absW[:, :])
                then(dve.tensor_scalar(odown_of(j), unscale[:, 2, :], hpow2[:, 0:1], 1.0 / ROOM, ALU.mult, ALU.mult))
                dve.tensor_tensor(blocks(hw), blocks(hw), each_block(dscale[:, :]), ALU.mult).then_inc(hd_ready, 1)

            def result_of(j):
                dve.wait_ge(residual_loaded, 16 * j + 16)
                dve.wait_ge(down_ready, j + 1)
                for n in range(HT):
                    cols = slice(n * P, (n + 1) * P)
                    last = dve.scalar_tensor_tensor(row_out[:, cols], down_bank(j)[:, cols], odown_of(j)[:, n:n + 1],
                                                    row_out[:, cols], ALU.mult, ALU.add)
                last.then_inc(down_taken, 1)

            turn(B, attention=False)

            def slot(r, result=True, last=False):
                def chunk(c):
                    hidden_of(4 * r + c, c % 2, h[:, r % RING, c * 512:(c + 1) * 512], unscale[:, 1, c:c + 1])

                if result:
                    result_of(r - (RING + 1))
                    dve.wait_ge(down_taken, r - RING)
                    round_hidden(r - RING)
                if not last:
                    stats_of_row(r + 1)
                chunk(0)
                hidden_lo(r - RING)
                chunk(1)
                if last:
                    all_of(scale_hidden(TAIL))
                    round_hidden(TAIL)
                    chunk(2)
                    all_of(scale_hidden(TAIL + 1))
                    chunk(3)
                else:
                    scale_row(r + 1)
                    chunk(2)
                    round_row(r + 1)
                    row_lo(r + 1)
                    chunk(3)
                    all_of(scale_hidden(r - (RING - 1)))

            @contextmanager
            def fori(first, end):
                with dve.Fori(first, end) as r:
                    own.enter(r - first, SLOT_STEPS)
                    yield r
                    own.leave(end - first)

            run_slots(slot, fori)
            third = scale_hidden(TAIL + 2)
            next(third)
            round_hidden(TAIL + 1)
            result_of(TAIL - 1)
            next(third)
            fourth = scale_hidden(TAIL + 3)
            next(fourth)
            result_of(TAIL)
            round_hidden(TAIL + 2)
            next(fourth)
            result_of(TAIL + 1)
            round_hidden(TAIL + 3)
            result_of(TAIL + 2)
            result_of(TAIL + 3)


def kernel(x, ctx_1024, L0_xattn_Wq, L0_xattn_bq, L0_xattn_Wk, L0_xattn_bk, L0_ffn_gate_w, L0_ffn_up_w, L0_ffn_down_w):
    import numpy as np
    import concourse.bacc as bacc
    from concourse.bass_utils import run_bass_kernel_spmd

    arrays = {
        "x": np.ascontiguousarray(x),
        "ctxT": np.ascontiguousarray(np.transpose(ctx_1024, (0, 2, 1))),
        "wqT": np.ascontiguousarray(np.transpose(L0_xattn_Wq)),
        "bq": np.ascontiguousarray(np.reshape(L0_xattn_bq, (-1, 1))),
        "wkT": np.ascontiguousarray(np.transpose(L0_xattn_Wk)),
        "bk": np.ascontiguousarray(np.reshape(L0_xattn_bk, (-1, 1))),
        "gate_w": np.ascontiguousarray(L0_ffn_gate_w),
        "up_w": np.ascontiguousarray(L0_ffn_up_w),
        "down_w": np.ascontiguousarray(L0_ffn_down_w),
        "ident": np.eye(P, dtype=np.float32),
    }
    nc = bacc.Bacc("TRN2", target_bir_lowering=False, num_devices=1)
    args = [nc.dram_tensor(f"in_{n}", a.shape, mybir.dt.from_np(a.dtype), kind="ExternalInput").ap()
            for n, a in arrays.items()]
    out = nc.dram_tensor("out_y", arrays["x"].shape, F32, kind="ExternalOutput").ap()
    xattn_ffn(nc, *args, out)
    r = run_bass_kernel_spmd(nc, [{f"in_{n}": a for n, a in arrays.items()}], core_ids=[0])
    return r.results[0]["out_y"]
```
